# Optimizing a Trainium2 kernel written in Bass

```python
import numpy as np
import jax
import jax.numpy as jnp

def _softmax(x, axis=-1):
    return jax.nn.softmax(x, axis=axis)

def _gelu(x):
    return jax.nn.gelu(x, approximate=True)

def _silu(x):
    return jax.nn.silu(x)

def _sigmoid(x):
    return jax.nn.sigmoid(x)

def _layernorm(x, axis=-1, eps=1e-05):
    m = jnp.mean(x, axis=axis, keepdims=True)
    v = jnp.var(x, axis=axis, keepdims=True)
    return (x - m) / jnp.sqrt(v + eps)

def _scatter_add(tgt, idx, src, axis=0):
    return tgt.at[idx].add(src)

def _segment_sum(src, seg, n):
    return jax.ops.segment_sum(src, seg, n)
kernel_name = 'mk_adj_resnorm_d2_adj_r2_b5d8fd'

def setup_inputs(seed: int=0):
    np.random.seed(seed)
    _w = jnp.asarray

    def _rec_inputs():
        import jax
        import jax.numpy as jnp
        _gk = jax.random.key(seed)
        x = 0.5 + 0.2887 * jax.random.normal(jax.random.fold_in(_gk, 1), (4096, 256), jnp.float32)
        _a = jax.random.bernoulli(jax.random.fold_in(_gk, 2), 0.000976562, (4096, 4096))
        _a = jnp.logical_or(_a, jnp.eye(4096, dtype=bool))
        _af = _a.astype(jnp.float32)
        _af = _af * jax.random.uniform(jax.random.fold_in(_gk, 3), (4096, 4096), jnp.float32, 0.05, 1)
        adj = _af
        return (x, adj)
    x, adj = _rec_inputs()

    def _L0_gnn_setup():
        import jax, jax.numpy as jnp
        import numpy as np
        N = 4096
        IN_C = 256
        OUT_C = 256
        key = jax.random.key(seed)
        k1, k2, k3 = jax.random.split(key, 3)
        adj_matrix = jax.random.uniform(k1, (N, N), dtype=jnp.float32)
        x = jax.random.uniform(k2, (N, IN_C), dtype=jnp.float32)
        weight = jax.random.uniform(k3, (IN_C, OUT_C), dtype=jnp.float32) / 4 - 0.125
        return {'x': x, 'adj_matrix': adj_matrix, 'weight': weight}
    _L0_gnn_all = _L0_gnn_setup()
    _L0_gnn_in = {k: v for k, v in _L0_gnn_all.items() if k in ('weight',)}
    del _L0_gnn_all

    def _L1_gnn_setup():
        import jax, jax.numpy as jnp
        import numpy as np
        N = 3072
        D_IN = 256
        D_OUT = 256
        DENSITY = 0.005
        key = jax.random.key(seed)
        ks = jax.random.split(key, 12)
        x = jax.random.normal(ks[0], (N, D_IN), dtype=jnp.float32)
        adj_a = (jax.random.uniform(ks[1], (N, N)) < DENSITY).astype(jnp.float32)
        adj_b = (jax.random.uniform(ks[2], (N, N)) < DENSITY).astype(jnp.float32)
        W_sa = jax.random.normal(ks[3], (D_IN, D_OUT), dtype=jnp.float32) * (1.414 / np.sqrt(D_IN + D_OUT))
        a_sa = jax.random.normal(ks[4], (1, 2 * D_OUT), dtype=jnp.float32) * (1.414 / np.sqrt(1 + 2 * D_OUT))
        stdv = 1.0 / np.sqrt(D_OUT)
        W_gcnb = jax.random.uniform(ks[5], (D_IN, D_OUT), minval=-stdv, maxval=stdv, dtype=jnp.float32)
        b_gcnb = jax.random.uniform(ks[6], (D_OUT,), minval=-stdv, maxval=stdv, dtype=jnp.float32)
        s = 1.0 / np.sqrt(2 * D_IN)
        Wa = jax.random.uniform(ks[7], (1, 2 * D_IN), minval=-s, maxval=s, dtype=jnp.float32)
        ba = jax.random.uniform(ks[8], (1,), minval=-s, maxval=s, dtype=jnp.float32)
        Wb = jax.random.uniform(ks[9], (1, 2 * D_IN), minval=-s, maxval=s, dtype=jnp.float32)
        bb = jax.random.uniform(ks[10], (1,), minval=-s, maxval=s, dtype=jnp.float32)
        return {'x': x, 'adj_a': adj_a, 'adj_b': adj_b, 'W_sa': W_sa, 'a_sa': a_sa, 'W_gcnb': W_gcnb, 'b_gcnb': b_gcnb, 'Wa': Wa, 'ba': ba, 'Wb': Wb, 'bb': bb}
    _L1_gnn_all = _L1_gnn_setup()
    _L1_gnn_in = {k: v for k, v in _L1_gnn_all.items() if k in ('W_sa', 'a_sa', 'W_gcnb', 'b_gcnb', 'Wa', 'ba', 'Wb', 'bb')}
    del _L1_gnn_all
    return {'x': x, 'adj': adj, 'L0_gnn_weight': _L0_gnn_in['weight'], 'L1_gnn_W_sa': _L1_gnn_in['W_sa'], 'L1_gnn_a_sa': _L1_gnn_in['a_sa'], 'L1_gnn_W_gcnb': _L1_gnn_in['W_gcnb'], 'L1_gnn_b_gcnb': _L1_gnn_in['b_gcnb'], 'L1_gnn_Wa': _L1_gnn_in['Wa'], 'L1_gnn_ba': _L1_gnn_in['ba'], 'L1_gnn_Wb': _L1_gnn_in['Wb'], 'L1_gnn_bb': _L1_gnn_in['bb']}

def reference(x, adj, L0_gnn_weight, L1_gnn_W_sa, L1_gnn_a_sa, L1_gnn_W_gcnb, L1_gnn_b_gcnb, L1_gnn_Wa, L1_gnn_ba, L1_gnn_Wb, L1_gnn_bb):
    import jax
    import jax.numpy as jnp

    def _L0_gnn_ref(x, adj_matrix, weight):
        import jax, jax.numpy as jnp
        import numpy as np
        N = 4096
        IN_C = 256
        OUT_C = 256
        n = adj_matrix.shape[0]
        deg = jnp.sum(adj_matrix, axis=1)
        dinv = (deg + 1.0) ** (-0.5)
        aug = dinv[:, None] * (adj_matrix + jnp.eye(n, dtype=adj_matrix.dtype)) * dinv[None, :]
        return jax.nn.relu(aug @ x @ weight)

    def _L1_gnn_ref(x, adj_a, adj_b, W_sa, a_sa, W_gcnb, b_gcnb, Wa, ba, Wb, bb):
        import jax, jax.numpy as jnp
        import numpy as np
        N = 3072
        D_IN = 256
        D_OUT = 256
        DENSITY = 0.005
        type_sum_a = adj_a @ x
        type_sum_b = adj_b @ x
        attn_a = jax.nn.sigmoid(jnp.concatenate([type_sum_a, x], axis=1) @ Wa.T + ba)
        attn_b = jax.nn.sigmoid(jnp.concatenate([type_sum_b, x], axis=1) @ Wb.T + bb)
        h = x @ W_sa
        Hd = h.shape[1]
        s_left = h @ a_sa[0, :Hd]
        s_right = h @ a_sa[0, Hd:]
        scores = s_left[:, None] + s_right[None, :]
        e = jnp.where(adj_a != 0, jnp.exp(-jax.nn.leaky_relu(scores, 0.01)), 0.0)
        attn = e / (jnp.sum(e, axis=1, keepdims=True) + 1e-05)
        x_a = attn @ h
        x_b = adj_b @ (x @ W_gcnb) + b_gcnb
        return jax.nn.sigmoid(attn_a * x_a + attn_b * x_b)
    x = _layernorm(x + _L0_gnn_ref(x, adj, L0_gnn_weight), axis=-1)
    x = _layernorm(x + _L1_gnn_ref(x, adj, adj, L1_gnn_W_sa, L1_gnn_a_sa, L1_gnn_W_gcnb, L1_gnn_b_gcnb, L1_gnn_Wa, L1_gnn_ba, L1_gnn_Wb, L1_gnn_bb), axis=-1)
    return x

_drawn_inputs = setup_inputs


def setup_inputs(seed=0):
    import zlib

    import numpy as np

    out = dict(_drawn_inputs(seed))
    spreads = {}
    factors = {'L1_gnn_a_sa': 8.0, 'L1_gnn_b_gcnb': 8.0, 'L1_gnn_Wa': 3.574}
    for name, (base, spread) in spreads.items():
        noise = np.random.default_rng([zlib.crc32(name.encode()), seed]).standard_normal(out[name].shape)
        drawn = base * np.exp(spread * noise) if base else spread * noise
        out[name] = jnp.asarray(drawn.astype(out[name].dtype))
    for name, factor in factors.items():
        out[name] = (out[name] * factor).astype(out[name].dtype)
    return out
```

```python
from contextlib import ExitStack

import concourse.bass as bass
from concourse import mybir

ALU = mybir.AluOpType
ACT = mybir.ActivationFunctionType
AX_X = mybir.AxisListType.X
F32 = mybir.dt.float32
F32R = mybir.dt.float32r
I32 = mybir.dt.int32

P = 128
QUADS = 4
QP = P // QUADS
STEPS = 32
CHUNKS = 8
RG = STEPS // CHUNKS
COLS = RG * P
TILES = CHUNKS
BLOCKS = COLS // QP
D = 256
PAIRS = CHUNKS // 2
EPS = 1e-5
SLOPE = 0.01
RSQRT_SEED = 0x5F3759DF
NEWTON = 3
ALL_UNITS = 2 * TILES
SLOTS = 3
SLOTS_AFTER = 2
SUMMED_BY = ("DDDDDDDD", "DAPDADPD", "PADAPADD", "PAPAPAPD")

PROJECT_AT = {16: (0, 1, 2, 3), 12: (0, 1, 2, 3), 8: (0, 0, 1, 1), 4: (0, 0, 1, 1)}
RESIDUAL_AT = {16: (1, 2, 3, 4), 12: (1, 2, 3, 4), 8: (1, 1, 2, 2), 4: (1, 1, 2, 2)}
NORM_AT = {16: 5, 12: 5, 8: 3, 4: 2}
SCORES_AT = {16: (7, 8, 9, 10), 12: (7, 8, 9, 10), 8: (4, 5, 5, 6), 4: (3, 3, 3, 3)}
TABLE_AT = {16: 11, 12: 11, 8: 7, 4: 3}
OUT_AT = (1, 4, 7, 10)


class Pass:

    def __init__(self, kind, q, tiles_loaded, tiles_used, unit0, tile0, pass0):
        self.kind, self.q = kind, q
        self.loaded, self.used = tiles_loaded, tiles_used
        self.units = 2 * len(tiles_used)
        self.slots = SLOTS if kind == "degree" else SLOTS_AFTER
        self.unit0, self.tile0, self.pass0 = unit0, tile0, pass0

    def unit(self, it, u):
        return self.unit0 + it * self.units + u

    def tile(self, it, k):
        return self.tile0 + it * len(self.loaded) + k

    def arrivals(self, it, k):
        slot = k % self.slots
        per_chunk = len(range(slot, len(self.loaded), self.slots))
        if self.kind == "degree":
            return (2 * self.q + it) * per_chunk + k // self.slots + 1
        degrees = CHUNKS * len(range(slot, TILES, SLOTS))
        return degrees + (self.tile0 - TILES * CHUNKS) // self.slots + it * per_chunk + k // self.slots + 1

    def step(self, u, j):
        return 4 * self.used[u // 2] + 2 * (u % 2) + j


def plan():
    unit = tile = done = 0
    degree, final = [], []
    for q in range(PAIRS):
        s = Pass("degree", q, list(range(TILES)), list(range(2 * q)), unit, tile, done)
        degree.append(s)
        unit, tile, done = unit + 2 * s.units, tile + 2 * TILES, done + 2 * (q > 0)
    for q in range(PAIRS):
        left = list(range(2 * q, TILES))
        s = Pass("final", q, left, left, unit, tile, done)
        final.append(s)
        unit, tile, done = unit + 2 * s.units, tile + 2 * len(left), done + 2
    attend = Pass("attend", 0, list(range(TILES)), list(range(TILES)), unit, tile, done)
    return degree, final, attend


def two_layers(nc, x, adj, w0, w_sa, a_sa, w_gc, b_gc, wa, ba, wb, bb, eye, fold, out):
    degree, final, attend = plan()
    LAYER1_PASSES = final[0].pass0

    with ExitStack() as ctx:
        def sb(name, shape, dt=F32):
            return ctx.enter_context(nc.sbuf_tensor(name, shape, dt))

        def psum(name):
            return ctx.enter_context(nc.psum_tensor(name, [P, 512], F32))

        def sem(name):
            return ctx.enter_context(nc.semaphore(name))

        nodes = sb("nodes", [P, STEPS, D])
        sta_hi = sb("sta_hi", [P, STEPS, D], F32R)
        sta_lo = sb("sta_lo", [P, STEPS, D], F32R)
        raw = sb("raw", [P, 2 * BLOCKS * P + P])
        adjt = sb("adjt", [P, 2, 2, COLS])
        adj_hi = sb("adj_hi", [P, 2, 2, COLS], F32R)
        adj_lo = sb("adj_lo", [P, 2, 2, COLS], F32R)
        e_hi = sb("e_hi", [P, 2, 2, COLS], F32R)
        e_lo = sb("e_lo", [P, 2, 2, COLS], F32R)
        room = sb("room", [P, CHUNKS, 2 * COLS])
        agg = sb("agg", [P, 2, COLS])
        eagg = sb("eagg", [P, 2, COLS])
        w0_sb = eagg[:, 0, :].rearrange("p (h n) -> p h n", h=2)
        a_row = eagg[:, 1, :].rearrange("p (h n) -> p h n", h=2)
        row_s = agg[:, 0, 0:D]
        wsa = sb("wsa", [P, 2, D + 1])
        sl_chunk = room[:, 4, COLS:2 * COLS]
        bias_g = room[:, 5, COLS:COLS + D]
        row_g = room[:, 5, COLS + D:COLS + 2 * D]
        wgc = room[:, 6:8, COLS:COLS + D + 2]
        row_gates = sb("row_gates", [P, 2])
        w4 = sb("w4", [P, 2, 4])
        wl_rep = sb("wl_rep", [P, 2, P])
        fold_sb = sb("fold_sb", [P, P])
        eye_sb = sb("eye_sb", [P, P])
        pick = sb("pick", [P, 3, P])
        bias_ab = sb("bias_ab", [P, 2])
        dinv = sb("dinv", [P, STEPS])
        degp1 = sb("degp1", [P, 8])
        seed = sb("seed", [P, 8], I32)
        tmp_d = sb("tmp_d", [P, 8])
        dinv_c = sb("dinv_c", [P, RG])
        relu_sb = sb("relu_sb", [P, 2, D])
        val = sb("val", [P, RG, D])
        deg_part = val[:, 0, 0:BLOCKS * TILES].rearrange("p (g t) -> p g t", g=BLOCKS)
        deg_sum = val[:, 1, 0:2 * BLOCKS].rearrange("p (i g) -> p i g", i=2)
        stats = sb("stats", [P, RG, 6])
        mv = sb("mv", [P, RG, 2])
        varc = sb("varc", [P, RG])
        rstd = sb("rstd", [P, RG])
        seed_v = sb("seed_v", [P, RG], I32)
        tmp_v = sb("tmp_v", [P, RG])
        shift = sb("shift", [P, RG])
        x1t = sb("x1t", [P, 2, 2, P])
        table = sb("table", [P, 4, STEPS])
        sl_scaled = sb("sl_scaled", [P, STEPS])
        tab_c = sb("tab_c", [P, RG, 3])
        gate = sb("gate", [P, RG, 7])
        mix = relu_sb
        zed = x1t[:].rearrange("p b h k -> p b (h k)")

        acc = [psum("acc_t0"), psum("acc_t1"), psum("acc_u0"), psum("acc_u1")]
        bank = [psum("bank4"), psum("bank5"), psum("bank6"), psum("bank7")]

        raw_full = [sem(f"raw_full{b}") for b in range(SLOTS)]
        read_out = [sem(f"read_out{b}") for b in range(SLOTS)]
        pool_sums = sem("pool_sums")
        deg_read = sem("deg_read")
        consts, x_in, late_in = sem("consts"), sem("x_in"), sem("late_in")
        late_setup = sem("late_setup")
        setup = sem("setup")
        deg_pair = sem("deg_pair")
        deg_folded = sem("deg_folded")
        dinv_done = sem("dinv_done")
        stahi_ready = sem("stahi_ready")
        sta_ready = sem("sta_ready")
        adjt_ready = sem("adjt_ready")
        hi_ready = sem("hi_ready")
        lo_ready = sem("lo_ready")
        pe_adj = sem("pe_adj")
        half0 = sem("half0")
        kept0, kept1 = sem("kept0"), sem("kept1")
        ex_mid = sem("ex_mid")
        ex_ready = sem("ex_ready")
        e_ready = sem("e_ready")
        ehi_ready = sem("ehi_ready")
        elo_ready = sem("elo_ready")
        pe_e = sem("pe_e")
        ehalf0 = sem("ehalf0")
        ekept0, ekept1 = sem("ekept0"), sem("ekept1")
        dinvc_ready = sem("dinvc_ready")
        proj = sem("proj")
        relu_done = sem("relu_done")
        sum_done = sem("sum_done")
        root_done = sem("root_done")
        norm_done = sem("norm_done")
        nodes_done = sem("nodes_done")
        xt_done = sem("xt_done")
        xt_kept = sem("xt_kept")
        dots_done = sem("dots_done")
        scores_kept = sem("scores_kept")
        table_done = sem("table_done")
        tabc_done = sem("tabc_done")
        floor_done = sem("floor_done")
        logit_done = sem("logit_done")
        gates_done = sem("gates_done")
        mixed = sem("mixed")
        mix_done = sem("mix_done")
        squashed = sem("squashed")
        stored = sem("stored")

        def exb(b):
            return room[:, 2 * b:2 * b + 2, COLS:2 * COLS]

        def eb(b):
            return exb(b)

        def reads(s, k):
            return 1 if k < 2 * s.q else 2

        def cols(t, r):
            return t.rearrange("p (a r k) -> p a r k", a=QUADS, r=RG)[:, :, r, :]

        def by_step(t):
            return t.rearrange("p (r a k) -> p a r k", a=QUADS, r=RG)

        def by_column(t):
            return t.rearrange("p (a r k) -> p a r k", a=QUADS, r=RG)

        def step_of(t, r):
            return t[:, r * P:(r + 1) * P]

        adj_v = adj.rearrange("(c g p) (t a j) -> a p c g t j", c=CHUNKS, p=QP, a=QUADS, t=TILES)
        x_v = x.rearrange("(c a r p) d -> a p c r d", a=QUADS, c=CHUNKS, r=RG)
        out_v = out.rearrange("(c a r p) d -> a p c r d", a=QUADS, c=CHUNKS, r=RG)
        raw_t = [raw[:, b * BLOCKS * P:(b + 1) * BLOCKS * P] for b in range(2)]
        raw_t.append(room[:, 0:2, :].rearrange("p c n -> p (c n)"))
        halved = agg[:].rearrange("p h n -> p (h n)").rearrange("p (g j) -> p g j", g=BLOCKS)

        block = ctx.enter_context(nc.Block())

        @block.sync
        def _(sp):
            late = [
                (wgc[:, :, 0:D], w_gc.rearrange("(h p) n -> p h n", h=2)),
                (row_g, w_gc[D - 1, :].partition_broadcast(P)),
                (bias_g, b_gc.partition_broadcast(P)),
            ]
            for g, w in enumerate((wa, wb)):
                w_v = w.rearrange("o (k h p) -> k h p o", k=2, h=2)
                for h in range(2):
                    late.append((wgc[:, h, D + g:D + g + 1], w_v[0, h]))

            def load_tile(s, k, chunk, after):
                t, slot = s.loaded[k], k % s.slots
                for a in range(QUADS):
                    src = adj_v[a][:, bass.ds(chunk, 1), :, t, :].rearrange("p o g j -> p (o g) j")
                    if a == 0 and after is not None:
                        sp.wait_ge(*after)
                    dst = raw_t[slot][QP * a:QP * a + QP].rearrange("p (g j) -> p g j", g=BLOCKS)
                    sp.dma_start(dst, src).then_inc(raw_full[slot], 16)

            def load_late():
                sp.wait_ge(kept1, attend.pass0)
                for dst, src in late:
                    sp.dma_start(dst, src).then_inc(late_in, 16)

            def load_pass(s, it, chunk, midway=None):
                def last_reader(k):
                    if s.kind == "degree":
                        if s.q == 0 and it == 0 and k < SLOTS:
                            return None
                        return read_out[k % SLOTS], sp.snap(2 * (s.arrivals(it, k) - 1))
                    if s is final[0] and it == 0 and k < 2:
                        return read_out[k], 2 * degree[PAIRS - 1].arrivals(1, TILES - SLOTS_AFTER + k)
                    return adjt_ready, sp.snap(s.unit(it, 0) + 2 * (k - 1))

                after = [last_reader(k) for k in range(len(s.loaded))]
                for k in range(len(s.loaded)):
                    if k == 2 and midway is not None:
                        midway()
                    load_tile(s, k, chunk, after[k])

            load_pass(degree[0], 0, 0)
            load_pass(degree[0], 1, 1)
            for s in degree[1:]:
                with sp.Fori(0, 2) as it:
                    load_pass(s, it, 2 * s.q + it)
            load_pass(final[0], 0, 0)
            load_pass(final[0], 1, 1)
            for s in final[1:]:
                with sp.Fori(0, 2) as it:
                    load_pass(s, it, 2 * s.q + it)

            def store(c, n_norm):
                for a in range(QUADS):
                    dst = out_v[a][:, bass.ds(c, 1), :, :].rearrange("p o r d -> p (o r) d")
                    if a == 0:
                        sp.wait_ge(norm_done, n_norm)
                    sp.dma_start(dst, val[QP * a:QP * a + QP]).then_inc(stored, 16)

            load_pass(attend, 0, 0, midway=load_late)
            load_pass(attend, 1, 1)
            with sp.Fori(2, CHUNKS) as c:
                n_norm = sp.snap(CHUNKS + c - 1)
                load_pass(attend, c, c, midway=lambda: store(c - 2, n_norm))
            store(CHUNKS - 2, 2 * CHUNKS - 1)
            store(CHUNKS - 1, 2 * CHUNKS)
            sp.wait_ge(stored, 16 * QUADS * CHUNKS)

        @block.tensor
        def _(pe):
            def product(s, u, it, moving_hi, moving_lo, banks, b, first_sem, done_sem):
                last_unit = u == s.units - 1
                for h in range(2):
                    if u == 0:
                        p = s.pass0 + it
                        if done_sem is pe_e:
                            p = it
                        if not (isinstance(p, int) and p == 0):
                            pe.wait_ge([kept0, kept1][h] if done_sem is pe_adj else [ekept0, ekept1][h], p)
                    for j in range(2):
                        st = s.step(u, j)
                        parts = ((sta_hi, moving_hi), (sta_lo, moving_hi), (sta_hi, moving_lo))
                        for k, (sta, mov) in enumerate(parts):
                            mm = pe.matmul(banks[h][:], sta[:, st, h * P:(h + 1) * P], mov[:, b, j, :],
                                           start=(u == 0 and j == 0 and k == 0),
                                           stop=(last_unit and j == 1 and k == 2))
                    if h == 0 and last_unit:
                        mm.then_inc(first_sem, 1)
                mm.then_inc(done_sem, 1)

            def adj_unit(s, it, u):
                pe.wait_ge(lo_ready, s.unit(it, u) + 1)
                product(s, u, it, adj_hi, adj_lo, acc[0:2], u % 2, half0, pe_adj)

            def project(c, r):
                f = RG * c + r
                if r == 0:
                    pe.wait_ge(kept0, LAYER1_PASSES + c + 1)
                    pe.wait_ge(kept1, LAYER1_PASSES + c + 1)
                if not (isinstance(f, int) and f < 2):
                    pe.wait_ge(relu_done, f - 1)
                for h in range(2):
                    mm = pe.matmul(bank[r % 2][:, 0:D], step_of(agg[:, h, :], r), w0_sb[:, h, :],
                                   start=(h == 0), stop=(h == 1))
                mm.then_inc(proj, 1)

            def scores(c, r):
                f = RG * c + r
                if r == 0:
                    pe.wait_ge(norm_done, c + 1)
                    if not isinstance(c, int) or c > 0:
                        pe.wait_ge(scores_kept, c)
                        pe.wait_ge(table_done, c)
                if not (isinstance(f, int) and f < 1):
                    pe.wait_ge(xt_kept, f)
                for h in range(2):
                    mm = pe.transpose(bank[2][:, h * P:(h + 1) * P], val[:, r, h * P:(h + 1) * P], eye_sb[:])
                mm.then_inc(xt_done, 1)
                pe.wait_ge(xt_kept, f + 1)
                for h in range(2):
                    pe.matmul(cols(bank[3][:], r), wl_rep[:, h, :], x1t[:, r % 2, h, :],
                              start=(h == 0), stop=(h == 1))
                for h in range(2):
                    mm = pe.matmul(bank[2][:, D + 4 * r:D + 4 * r + 4], x1t[:, r % 2, h, :], w4[:, h, :],
                                   start=(h == 0), stop=(h == 1))
                mm.then_inc(dots_done, 1)

            def project_out(c, r):
                f = RG * c + r
                if r == 0:
                    pe.wait_ge(kept0, attend.pass0 + c + 1)
                    pe.wait_ge(kept1, attend.pass0 + c + 1)
                    pe.wait_ge(ekept0, c + 1)
                    pe.wait_ge(ekept1, c + 1)
                if isinstance(f, int) and f < 2:
                    pe.wait_ge(late_setup, 1)
                    pe.wait_ge(relu_done, RG * CHUNKS)
                    pe.wait_ge(scores_kept, CHUNKS)
                    pe.wait_ge(table_done, CHUNKS)
                else:
                    pe.wait_ge(mix_done, f - 1)
                for src, w, n, b in ((agg, wgc, D + 2, r % 2), (eagg, wsa, D + 1, 2 + r % 2)):
                    for h in range(2):
                        mm = pe.matmul(bank[b][:, 0:n], step_of(src[:, h, :], r), w[:, h, :],
                                       start=(h == 0), stop=(h == 1))
                mm.then_inc(proj, 1)

            def degree_chunk(s, it):
                for u in range(s.units):
                    if u == 4 * (s.q - 1):
                        pe.wait_ge(sta_ready, s.q)
                    adj_unit(s, it, u)

            for s in degree:
                if s.q == 1:
                    degree_chunk(s, 0)
                    degree_chunk(s, 1)
                elif s.units:
                    with pe.Fori(0, 2) as it:
                        degree_chunk(s, it)
                pe.wait_ge(deg_pair, s.q + 1)
                if s.q == 0:
                    pe.wait_ge(consts, N_CONSTS)
                pe.matmul(bank[3][:, 0:2 * BLOCKS], fold_sb[:], deg_sum.rearrange("p i g -> p (i g)"),
                          start=True, stop=True).then_inc(deg_folded, 1)

            def final_chunk(s, it, prev):
                for u in range(s.units):
                    adj_unit(s, it, u)
                    for r in range(RG):
                        if prev is not None and PROJECT_AT[s.units][r] == u:
                            project(prev, r)
                    for r in range(RG):
                        if prev is not None and SCORES_AT[s.units][r] == u:
                            scores(prev, r)

            pe.wait_ge(sta_ready, PAIRS)
            pe.wait_ge(setup, 1)
            final_chunk(final[0], 0, None)
            final_chunk(final[0], 1, 0)
            for s in final[1:3]:
                with pe.Fori(0, 2) as it:
                    final_chunk(s, it, 2 * s.q + it - 1)
            final_chunk(final[3], 0, 5)
            final_chunk(final[3], 1, 6)

            def attend_chunk(c, tail):
                for u in range(attend.units):
                    if isinstance(c, int) and c == 0 and u % 4 == 0:
                        pe.wait_ge(sta_ready, PAIRS + u // 4 + 1)
                    adj_unit(attend, c, u)
                    pe.wait_ge(elo_ready, ALL_UNITS * c + u + 1)
                    product(attend, u, c, e_hi, e_lo, acc[2:4], u % 2, ehalf0, pe_e)
                    for r in range(RG):
                        if tail == "layer one" and PROJECT_AT[attend.units][r] == u:
                            project(CHUNKS - 1, r)
                        if tail == "layer one" and SCORES_AT[attend.units][r] == u:
                            scores(CHUNKS - 1, r)
                        if tail == "layer two" and OUT_AT[r] == u:
                            project_out(c - 1, r)

            attend_chunk(0, "layer one")
            attend_chunk(1, "layer two")
            with pe.Fori(2, CHUNKS) as c:
                attend_chunk(c, "layer two")
            for r in range(RG):
                project_out(CHUNKS - 1, r)

        @block.vector
        def _(dve):
            def settle(dst, src, op_seed, a, b):
                dve.tensor_scalar(a, src, 1, None, ALU.logical_shift_right)
                dve.drain()
                dve.tensor_scalar(b, a, -1.0, float(RSQRT_SEED), ALU.mult, ALU.add)

            def transpose_unit(s, it, u, diagonal):
                n = s.unit(it, u)
                k = u // 2 if u < s.units else len(s.loaded)
                slot = k % s.slots
                if u % 2 == 0:
                    dve.wait_ge(raw_full[slot], 64 * s.arrivals(it, k))
                if diagonal is not None:
                    for a in range(QUADS):
                        at = slot * BLOCKS * P + RG * a * P
                        d = raw[QP * a:QP * a + QP, at:at + RG * (P + QP)].rearrange(
                            "p (r j) -> p r j", r=RG)[:, :, 0:QP]
                        i = pick[QP * a:QP * a + QP, bass.ds(diagonal, 1), :].rearrange(
                            "p o (r j) -> p (o r) j", r=RG)
                        dve.tensor_tensor(d, d, i, ALU.add)
                    dve.drain()
                if not (isinstance(n, int) and n < 2):
                    dve.wait_ge(hi_ready, n - 1)
                    dve.wait_ge(lo_ready, n - 1)
                if s.kind == "attend":
                    m = ALL_UNITS * it + u
                    if not (isinstance(m, int) and m < 2):
                        dve.wait_ge(e_ready, m - 1)
                src = raw_t[slot].rearrange("p (g s j) -> p s g j", g=BLOCKS, s=RG)[:, 2 * (u % 2):2 * (u % 2) + 2]
                dve.transpose(adjt[:, u % 2].rearrange("p s (g i) -> p s g i", i=QP), src).then_inc(adjt_ready, 1)
                if s.kind == "degree" and u % 2:
                    dve.drain()
                    dve.nop().then_inc(read_out[slot], 1)

            def low_part(s, it, u):
                n = s.unit(it, u)
                dve.wait_ge(hi_ready, n + 1)
                if not (isinstance(n, int) and n < 2):
                    dve.wait_ge(pe_adj, n - 1)
                b = u % 2
                dve.tensor_tensor(adj_lo[:, b], adjt[:, b], adj_hi[:, b].bitcast(F32), ALU.subtract).then_inc(lo_ready, 1)

            def masked(c, u):
                n, b = ALL_UNITS * c + u, u % 2
                dve.wait_ge(ex_ready, 2 * (n + 1))
                dve.wait_ge(adjt_ready, attend.unit(c, u) + 1)
                if not (isinstance(n, int) and n < 2):
                    dve.wait_ge(ehi_ready, n - 1)
                    dve.wait_ge(elo_ready, n - 1)
                dve.scalar_tensor_tensor(out=eb(b), in0=adjt[:, b], scalar=0.0, in1=exb(b),
                                         op0=ALU.not_equal, op1=ALU.mult).then_inc(e_ready, 1)

            def e_low(c, u):
                n, b = ALL_UNITS * c + u, u % 2
                dve.wait_ge(ehi_ready, n + 1)
                if not (isinstance(n, int) and n < 2):
                    dve.wait_ge(pe_e, n - 1)
                dve.tensor_tensor(e_lo[:, b], eb(b), e_hi[:, b].bitcast(F32), ALU.subtract).then_inc(elo_ready, 1)

            def newton(v, y, t):
                for _ in range(NEWTON):
                    dve.scalar_tensor_tensor(out=t, in0=y, scalar=-0.5, in1=y, op0=ALU.mult, op1=ALU.mult)
                    dve.drain()
                    dve.tensor_tensor(t, t, v, ALU.mult)
                    dve.drain()
                    dve.scalar_tensor_tensor(out=y, in0=t, scalar=1.5, in1=y, op0=ALU.add, op1=ALU.mult)
                    dve.drain()

            def degree_chunk(s, it):
                for u in range(min(2, s.units)):
                    transpose_unit(s, it, u, None)
                for k in range(TILES):
                    if k < 2 * s.q:
                        for u in (2 * k, 2 * k + 1):
                            low_part(s, it, u)
                            if u + 2 < s.units:
                                transpose_unit(s, it, u + 2, None)
                    if SUMMED_BY[s.q][k] == "D":
                        dve.wait_ge(raw_full[k % SLOTS], 64 * s.arrivals(it, k))
                        dve.tensor_reduce(deg_part[:, :, k], raw_t[k % SLOTS].rearrange("p (g j) -> p g j", g=BLOCKS),
                                          AX_X, ALU.add).then_inc(read_out[k % SLOTS], reads(s, k))
                for k in range(TILES - SLOTS, TILES):
                    dve.wait_ge(read_out[k % SLOTS], 2 * s.arrivals(it, k))
                if s.q:
                    before = 2 * "".join(SUMMED_BY[:s.q]).count("P")
                    dve.wait_ge(pool_sums, before + (it + 1) * SUMMED_BY[s.q].count("P"))
                dve.wait_ge(consts, N_CONSTS)
                dve.tensor_reduce(deg_sum[:, bass.ds(it, 1), :].rearrange("p o g -> p (o g)"), deg_part,
                                  AX_X, ALU.add).then_inc(deg_read, 1)
                dve.drain()
                if s.units:
                    dve.wait_ge(half0, s.pass0 + it + 1)
                    dve.wait_ge(consts, N_CONSTS)
                    kept = room[:, bass.ds(2 * s.q + it, 1), :].rearrange("p o n -> p (o n)")
                    dve.tensor_copy(kept[:, 0:COLS], acc[0][:]).then_inc(kept0, 1)
                    dve.wait_ge(pe_adj, s.unit(it, s.units))
                    dve.wait_ge(consts, N_CONSTS)
                    dve.tensor_copy(kept[:, COLS:2 * COLS], acc[1][:]).then_inc(kept1, 1)

            for s in degree:
                if s.q == 1:
                    degree_chunk(s, 0)
                    degree_chunk(s, 1)
                else:
                    with dve.Fori(0, 2) as it:
                        degree_chunk(s, it)
                dve.drain()
                dve.nop().then_inc(deg_pair, 1)
                dve.wait_ge(deg_folded, s.q + 1)
                for a in range(QUADS):
                    rows = slice(QP * a, QP * a + QP)
                    dve.tensor_scalar(degp1[rows].rearrange("p (i r) -> p i r", i=2),
                                      bank[3][rows, 0:2 * BLOCKS].rearrange("p (i g) -> p i g", i=2)[:, :, RG * a:RG * a + RG],
                                      1.0, None, ALU.add)
                dve.drain()
                dv = dinv[:, 8 * s.q:8 * s.q + 8]
                settle(dv, degp1[:].bitcast(I32), RSQRT_SEED, seed[:], dv.bitcast(I32))
                dve.drain()
                newton(degp1[:], dv, tmp_d[:])
                dve.wait_ge(x_in, 16 * QUADS * CHUNKS)
                dve.nop().then_inc(dinv_done, 1)
                for st in range(8 * s.q, 8 * s.q + 8):
                    dve.wait_ge(stahi_ready, st + 1)
                    ins = dve.scalar_tensor_tensor(out=sta_lo[:, st, :], in0=nodes[:, st, :], scalar=dinv[:, st:st + 1],
                                                   in1=sta_hi[:, st, :].bitcast(F32), op0=ALU.mult, op1=ALU.subtract)
                ins.then_inc(sta_ready, 1)
                if s.q == 0:
                    dve.tensor_copy(pick[:, 0, :], fold_sb[:])
                    dve.memset(pick[:, 1, :], 0.0)
                    dve.tensor_copy(pick[:, 2, :], fold_sb[:])
                    for h in range(2):
                        for side, col in ((1, 0), (0, 1)):
                            dve.tensor_tensor_reduce(out=relu_sb[:, 0, :], in0=wsa[:, h, 0:D], in1=a_row[:, side, :],
                                                     scale=1.0, scalar=0.0, op0=ALU.mult, op1=ALU.add,
                                                     accum_out=w4[:, h, col:col + 1])
                            dve.drain()
                        dve.tensor_scalar(wl_rep[:, h, :], fold_sb[:], 0.0, w4[:, h, 1:2], ALU.mult, ALU.add)
                        dve.tensor_tensor(wsa[:, h, 0:D], wsa[:, h, 0:D], row_s, ALU.subtract)
                    dve.memset(wsa[:, 0, D:D + 1], 0.0)
                    dve.tensor_copy(wsa[:, 1, D:D + 1], eye_sb[:, P - 1:P])
                    dve.drain()
                    dve.nop().then_inc(setup, 1)

            def chunk_statistics():
                dve.drain()
                dve.tensor_scalar(varc[:], mv[:, :, 1], EPS, None, ALU.add)
                dve.drain()
                settle(rstd, varc[:].bitcast(I32), RSQRT_SEED, seed_v[:], rstd[:].bitcast(I32))
                dve.drain()
                newton(varc[:], rstd[:], tmp_v[:])
                dve.scalar_tensor_tensor(out=shift[:], in0=mv[:, :, 0], scalar=-1.0, in1=rstd[:],
                                         op0=ALU.mult, op1=ALU.mult).then_inc(root_done, 1)

            def row_statistics(f, r):
                dve.wait_ge(sum_done, f + 1)
                dve.bn_stats(stats[:, r, :], val[:, r, :])
                dve.drain()
                dve.bn_aggr(mv[:, r, :], stats[:, r, :])

            def chunk_dinv(c):
                if not (isinstance(c, int) and c == 0):
                    dve.wait_ge(relu_done, RG * c)
                dve.tensor_copy(dinv_c[:], dinv[:, bass.ds(RG * c, RG)]).then_inc(dinvc_ready, 1)

            def residual(c, r):
                if r == 0 and not (isinstance(c, int) and c == 0):
                    dve.wait_ge(norm_done, c)
                row_statistics(RG * c + r, r)
                if r == RG - 1:
                    chunk_statistics()

            def keep_table(c):
                dve.wait_ge(dots_done, RG * c + RG)
                dve.wait_ge(setup, 1)
                dots = bank[2][:, D:D + 4 * RG].rearrange("p (r k) -> p k r", r=RG)
                dve.tensor_copy(table[:, :, bass.ds(RG * c, RG)], dots)
                dve.tensor_scalar(sl_scaled[:, bass.ds(RG * c, RG)], dots[:, 0, :], -SLOPE, None, ALU.mult).then_inc(table_done, 1)

            def sta_of_x1(q):
                dve.wait_ge(nodes_done, 2 * q + 2)
                dve.wait_ge(pe_adj, final[q].unit(1, final[q].units))
                rows = slice(8 * q, 8 * q + 8)
                dve.tensor_copy(sta_hi[:, rows, :], nodes[:, rows, :])
                dve.drain()
                dve.tensor_tensor(sta_lo[:, rows, :], nodes[:, rows, :], sta_hi[:, rows, :].bitcast(F32), ALU.subtract)
                dve.drain()
                dve.tensor_scalar(sta_hi[:, rows, D - 1], nodes[:, rows, D - 1], 0.0, 1.0, ALU.mult, ALU.add)
                dve.tensor_scalar(sta_lo[:, rows, D - 1], nodes[:, rows, D - 1], 0.0, None, ALU.mult).then_inc(sta_ready, 1)

            def tail_one(prev, u, units):
                if PROJECT_AT[units][0] == u:
                    chunk_dinv(prev)
                for r in range(RG):
                    if RESIDUAL_AT[units][r] == u:
                        residual(prev, r)

            def final_chunk(s, it, prev, head, next_pick):
                if head:
                    transpose_unit(s, it, 0, it)
                    transpose_unit(s, it, 1, None)
                    low_part(s, it, 0)
                for u in range(s.units):
                    if u:
                        low_part(s, it, u)
                    if u + 2 < s.units:
                        transpose_unit(s, it, u + 2, 1 + it if u == 0 else None)
                    elif s.q == 3 and next_pick is None:
                        transpose_unit(attend, 0, u + 2 - s.units, None)
                    else:
                        transpose_unit(s, it, u + 2, next_pick if u + 2 == s.units else None)
                    if prev is not None:
                        tail_one(prev, u, s.units)
                        if TABLE_AT[s.units] == u and u < s.units - 1:
                            keep_table(prev)
                if s.q == 3 and next_pick is None:
                    low_part(attend, 0, 0)
                else:
                    low_part(s, it, s.units)
                dve.wait_ge(half0, s.pass0 + it + 1)
                if prev is not None or s.q:
                    dve.wait_ge(proj, RG * (2 * s.q + it))
                c = 2 * s.q + it
                part = room[:, bass.ds(c, 1), :].rearrange("p o n -> p (o n)")
                if s.q:
                    dve.tensor_tensor(by_step(agg[:, 0, :]), by_column(acc[0][:]), by_column(part[:, 0:COLS]), ALU.add).then_inc(kept0, 1)
                else:
                    dve.tensor_copy(by_step(agg[:, 0, :]), by_column(acc[0][:])).then_inc(kept0, 1)
                dve.wait_ge(pe_adj, s.unit(it, s.units))
                if s.q:
                    dve.tensor_tensor(by_step(agg[:, 1, :]), by_column(acc[1][:]), by_column(part[:, COLS:2 * COLS]), ALU.add).then_inc(kept1, 1)
                else:
                    dve.tensor_copy(by_step(agg[:, 1, :]), by_column(acc[1][:])).then_inc(kept1, 1)
                if prev is not None and TABLE_AT[s.units] == s.units - 1:
                    keep_table(prev)

            final_chunk(final[0], 0, None, True, 1)
            final_chunk(final[0], 1, 0, False, 0)
            for s in final[1:3]:
                with dve.Fori(0, 2) as it:
                    final_chunk(s, it, 2 * s.q + it - 1, False, 1 + it)
                sta_of_x1(s.q - 1)
            final_chunk(final[3], 0, 5, False, 1)
            final_chunk(final[3], 1, 6, False, None)
            sta_of_x1(2)

            def gates_in(c, r):
                f = RG * c + r
                if r == 0:
                    if not (isinstance(c, int) and c == 0):
                        dve.wait_ge(gates_done, RG * c)
                    dve.tensor_tensor(tab_c[:, :, 1:3], table[:, 2:4, bass.ds(RG * c, RG)].rearrange("p k r -> p r k"),
                                      bias_ab[:].unsqueeze(1).broadcast_to((P, RG, 2)), ALU.add)
                    dve.tensor_copy(tab_c[:, :, 0], table[:, 1, bass.ds(RG * c, RG)])
                    dve.drain()
                    dve.nop().then_inc(tabc_done, 1)
                dve.wait_ge(proj, RG * (CHUNKS + c) + r + 1)
                dve.tensor_tensor(gate[:, r, 0:2], bank[r % 2][:, D:D + 2], tab_c[:, r, 1:3], ALU.add).then_inc(logit_done, 1)

            def mix_in(c, r):
                f = RG * c + r
                dve.wait_ge(gates_done, f + 1)
                dve.tensor_scalar(gate[:, r, 0:2], gate[:, r, 2:4], 0.5, 0.5, ALU.mult, ALU.add)
                dve.scalar_tensor_tensor(out=gate[:, r, 4:5], in0=tab_c[:, r, 0:1], scalar=EPS,
                                         in1=bank[2 + r % 2][:, D:D + 1], op0=ALU.mult, op1=ALU.add)
                dve.drain()
                dve.reciprocal(gate[:, r, 5:6], gate[:, r, 4:5])
                dve.drain()
                dve.tensor_tensor(gate[:, r, 6:7], gate[:, r, 5:6], gate[:, r, 0:1], ALU.mult)
                if not (isinstance(f, int) and f < 2):
                    dve.wait_ge(squashed, f - 1)
                dve.tensor_tensor(mix[:, r % 2, :], bank[r % 2][:, 0:D], bias_g, ALU.add)
                dve.drain()
                dve.tensor_scalar(mix[:, r % 2, :], mix[:, r % 2, :], gate[:, r, 1:2], None, ALU.mult)
                dve.drain()
                dve.scalar_tensor_tensor(out=mix[:, r % 2, :], in0=bank[2 + r % 2][:, 0:D], scalar=gate[:, r, 6:7],
                                         in1=mix[:, r % 2, :], op0=ALU.mult, op1=ALU.add).then_inc(mix_done, 1)

            def norm_in(c, r):
                if r == 0:
                    dve.wait_ge(norm_done, CHUNKS + c)
                row_statistics(RG * (CHUNKS + c) + r, r)
                if r == RG - 1:
                    chunk_statistics()

            def attend_chunk(c, tail, more):
                if isinstance(c, int) and c == 0:
                    masked(c, 0)
                for u in range(attend.units):
                    if u == 0:
                        e_low(c, u)
                        transpose_unit(attend, c, u + 2, None)
                    else:
                        masked(c, u)
                        low_part(attend, c, u)
                        if u + 2 < attend.units or more:
                            transpose_unit(attend, c, u + 2, None)
                        e_low(c, u)
                    if tail == "layer one":
                        tail_one(CHUNKS - 1, u, attend.units)
                        if u == TABLE_AT[attend.units]:
                            keep_table(CHUNKS - 1)
                            sta_of_x1(PAIRS - 1)
                    if tail == "layer two":
                        for r in range(RG):
                            if u == OUT_AT[r] + 1:
                                gates_in(c - 1, r)
                            if u == OUT_AT[r] + 2:
                                mix_in(c - 1, r)
                            if u == OUT_AT[r] + 3:
                                norm_in(c - 1, r)
                if more:
                    masked(c, attend.units)
                    low_part(attend, c, attend.units)
                dve.wait_ge(pe_adj, attend.unit(c, attend.units))
                dve.wait_ge(proj, RG * (CHUNKS + c))
                dve.tensor_copy(by_step(agg[:, 1, :]), by_column(acc[1][:])).then_inc(kept1, 1)
                dve.wait_ge(pe_e, ALL_UNITS * (c + 1))
                dve.tensor_copy(by_step(eagg[:, 1, :]), by_column(acc[3][:])).then_inc(ekept1, 1)

            attend_chunk(0, "layer one", True)
            dve.wait_ge(late_in, N_LATE)
            for h in range(2):
                dve.tensor_tensor(wgc[:, h, 0:D], wgc[:, h, 0:D], row_g, ALU.subtract)
                dve.tensor_tensor(wgc[:, h, D:D + 2], wgc[:, h, D:D + 2], row_gates[:], ALU.subtract)
            dve.drain()
            dve.nop().then_inc(late_setup, 1)
            attend_chunk(1, "layer two", True)
            with dve.Fori(2, CHUNKS - 1) as c:
                attend_chunk(c, "layer two", True)
            attend_chunk(CHUNKS - 1, "layer two", False)
            for r in range(RG):
                gates_in(CHUNKS - 1, r)
                mix_in(CHUNKS - 1, r)
                norm_in(CHUNKS - 1, r)

        @block.scalar
        def _(act):
            act.preload_act_table(ACT.Exp)
            with act.Fori(0, CHUNKS) as c:
                for a in range(QUADS):
                    act.dma_start(nodes[QP * a:QP * a + QP, bass.ds(RG * c, RG), :],
                                  x_v[a][:, bass.ds(c, 1)].rearrange("p o r d -> p (o r) d")).then_inc(x_in, 16)
            small = [
                (fold_sb[:], fold), (eye_sb[:], eye),
                (w0_sb, w0.rearrange("(h p) n -> p h n", h=2)),
                (wsa[:, :, 0:D], w_sa.rearrange("(h p) n -> p h n", h=2)),
                (row_s, w_sa[D - 1, :].partition_broadcast(P)),
                (a_row, a_sa.rearrange("o (h n) -> o h n", h=2)[0].partition_broadcast(P)),
                (bias_ab[:, 0:1], ba.partition_broadcast(P)),
                (bias_ab[:, 1:2], bb.partition_broadcast(P)),
            ]
            for g, w in enumerate((wa, wb)):
                w_v = w.rearrange("o (k h p) -> k h p o", k=2, h=2)
                small.append((row_gates[:, g:g + 1], w[0, D - 1:D].partition_broadcast(P)))
                for h in range(2):
                    small.append((w4[:, h, 2 + g:3 + g], w_v[1, h]))
            for dst, src in small:
                act.dma_start(dst, src).then_inc(consts, 16)

            unread = [bank[b][:, g * P:(g + 1) * P] for b in range(3) for g in range(4)]
            unread += [x1t[:, b, h, :] for b in range(2) for h in range(2)]

            def high_part(s, it, u):
                n, b = s.unit(it, u), u % 2
                act.wait_ge(adjt_ready, n + 1)
                if not (isinstance(n, int) and n < 2):
                    act.wait_ge(pe_adj, n - 1)
                act.activation(adj_hi[:, b], adjt[:, b], ACT.Copy).then_inc(hi_ready, 1)

            def degree_chunk(s, it):
                for k in range(TILES):
                    for half in range(2):
                        if k < 2 * s.q:
                            high_part(s, it, 2 * k + half)
                        if SUMMED_BY[s.q][k] == "A":
                            act.wait_ge(deg_read, 2 * s.q + it)
                            act.wait_ge(raw_full[k % SLOTS], 64 * s.arrivals(it, k))
                            rows = raw_t[k % SLOTS].rearrange("p (g j) -> p g j", g=BLOCKS)
                            for g in range(half * BLOCKS // 2, (half + 1) * BLOCKS // 2):
                                ins = act.activation(unread[g], rows[:, g, :], ACT.Copy, accum_out=deg_part[:, g, k:k + 1])
                            if half:
                                ins.then_inc(read_out[k % SLOTS], reads(s, k))
                                act.drain()

            act.wait_ge(x_in, 16 * QUADS * CHUNKS)
            for s in degree:
                if s.q == 1:
                    degree_chunk(s, 0)
                    degree_chunk(s, 1)
                elif s.q:
                    with act.Fori(0, 2) as it:
                        degree_chunk(s, it)
                act.wait_ge(dinv_done, s.q + 1)
                for st in range(8 * s.q, 8 * s.q + 8):
                    act.activation(sta_hi[:, st, :], nodes[:, st, :], ACT.Copy,
                                   scale=dinv[:, st:st + 1]).then_inc(stahi_ready, 1)

            def relu(c, r):
                f = RG * c + r
                act.wait_ge(proj, f + 1)
                if r == 0:
                    act.wait_ge(dinvc_ready, c + 1)
                if not (isinstance(f, int) and f < 2):
                    act.wait_ge(sum_done, f - 1)
                act.activation(relu_sb[:, r % 2, :], bank[r % 2][:, 0:D], ACT.Relu,
                               scale=dinv_c[:, r:r + 1]).then_inc(relu_done, 1)

            def keep_x1t(c, r):
                f = RG * c + r
                act.wait_ge(xt_done, f + 1)
                if not (isinstance(f, int) and f < 2):
                    act.wait_ge(dots_done, f - 1)
                act.activation(x1t[:, r % 2], bank[2][:, 0:D].rearrange("p (h k) -> p h k", h=2),
                               ACT.Copy).then_inc(xt_kept, 1)

            def keep_scores(c):
                act.wait_ge(dots_done, RG * c + RG)
                act.wait_ge(setup, 1)
                act.activation(room[:, bass.ds(c, 1), 0:COLS].rearrange("p o n -> p (o n)"), bank[3][:],
                               ACT.Copy).then_inc(scores_kept, 1)

            def normalise(count):
                act.wait_ge(root_done, count)
                for r in range(RG):
                    ins = act.activation(val[:, r, :], val[:, r, :], ACT.Identity, bias=shift[:, r:r + 1],
                                         scale=rstd[:, r:r + 1])
                ins.then_inc(norm_done, 1)

            def tail_one(prev, u, units):
                for r in range(RG):
                    if PROJECT_AT[units][r] == u:
                        relu(prev, r)
                if NORM_AT[units] == u:
                    normalise(prev + 1)
                for r in range(RG):
                    if SCORES_AT[units][r] == u:
                        keep_x1t(prev, r)
                if TABLE_AT[units] == u:
                    keep_scores(prev)

            def final_chunk(s, it, prev, head, more):
                if head:
                    high_part(s, it, 0)
                for u in range(s.units):
                    if u + 1 < s.units:
                        high_part(s, it, u + 1)
                    elif more:
                        n = s.unit(it, s.units)
                        act.wait_ge(adjt_ready, n + 1)
                        act.wait_ge(pe_adj, n - 1)
                        act.activation(adj_hi[:, 0], adjt[:, 0], ACT.Copy).then_inc(hi_ready, 1)
                    if prev is not None:
                        tail_one(prev, u, s.units)

            final_chunk(final[0], 0, None, True, True)
            final_chunk(final[0], 1, 0, False, True)
            for s in final[1:3]:
                with act.Fori(0, 2) as it:
                    final_chunk(s, it, 2 * s.q + it - 1, False, True)
            final_chunk(final[3], 0, 5, False, True)
            final_chunk(final[3], 1, 6, False, True)

            def next_scores(c):
                act.wait_ge(scores_kept, min(c, CHUNKS) + 1 if isinstance(c, int) else c + 1)
                if not (isinstance(c, int) and c == 0):
                    act.wait_ge(ex_mid, 2 * ALL_UNITS * c)
                act.wait_ge(setup, 1)
                act.activation(sl_chunk, room[:, bass.ds(c, 1), 0:COLS].rearrange("p o n -> p (o n)"), ACT.Copy)
                act.drain()

            def exponent(n, b, steps):
                if not (isinstance(n, int) and n < 2):
                    act.wait_ge(elo_ready, n - 1)
                for j, st in enumerate(steps):
                    act.activation(exb(b)[:, j, :], sl_chunk, ACT.Relu, bias=table[:, 0, st:st + 1]).then_inc(ex_mid, 1)
                act.wait_ge(ex_mid, 2 * (n + 1))
                for j, st in enumerate(steps):
                    act.activation(exb(b)[:, j, :], exb(b)[:, j, :], ACT.Exp, bias=sl_scaled[:, st:st + 1],
                                   scale=-(1 - SLOPE)).then_inc(ex_ready, 1)

            def e_high(c, u):
                n, b = ALL_UNITS * c + u, u % 2
                act.wait_ge(e_ready, n + 1)
                if not (isinstance(n, int) and n < 2):
                    act.wait_ge(pe_e, n - 1)
                act.activation(e_hi[:, b], eb(b), ACT.Copy).then_inc(ehi_ready, 1)

            def gates(c, r):
                f = RG * c + r
                if r == 0:
                    act.wait_ge(tabc_done, c + 1)
                    act.activation(tab_c[:, :, 0], tab_c[:, :, 0], ACT.Exp, scale=SLOPE)
                act.wait_ge(logit_done, f + 1)
                act.activation(gate[:, r, 2:4], gate[:, r, 0:2], ACT.Tanh, scale=0.5).then_inc(gates_done, 1)

            def squash(c, r):
                f = RG * c + r
                act.wait_ge(mix_done, f + 1)
                if not (isinstance(f, int) and f < 2):
                    act.wait_ge(sum_done, RG * CHUNKS + f - 1)
                act.activation(zed[:, r % 2, :], mix[:, r % 2, :], ACT.Tanh, scale=0.5)
                act.drain()
                act.activation(zed[:, r % 2, :], zed[:, r % 2, :], ACT.Copy, scale=0.5,
                               bias=0.5).then_inc(squashed, 1)

            def attend_chunk(c, tail, more):
                for u in range(attend.units):
                    e_high(c, u)
                    if u + 1 < attend.units:
                        exponent(ALL_UNITS * c + u + 1, (u + 1) % 2, [attend.step(u + 1, j) for j in range(2)])
                        high_part(attend, c, u + 1)
                    elif more:
                        next_scores(c + 1)
                        exponent(ALL_UNITS * (c + 1), 0, [attend.step(0, j) for j in range(2)])
                        high_part(attend, c + 1, 0)
                    if tail == "layer one":
                        tail_one(CHUNKS - 1, u, attend.units)
                    if tail == "layer two":
                        for r in range(RG):
                            if u == OUT_AT[r] + 1:
                                gates(c - 1, r)
                            if u == OUT_AT[r] + 2:
                                squash(c - 1, r)
                        if u == attend.units - 1:
                            normalise(CHUNKS + c)
                p = attend.pass0 + c + 1
                act.wait_ge(half0, p)
                act.wait_ge(proj, RG * (CHUNKS + c))
                act.activation(by_step(agg[:, 0, :]), by_column(acc[0][:]), ACT.Copy).then_inc(kept0, 1)
                act.wait_ge(ehalf0, c + 1)
                act.activation(by_step(eagg[:, 0, :]), by_column(acc[2][:]), ACT.Copy).then_inc(ekept0, 1)

            act.wait_ge(kept1, attend.pass0)
            next_scores(0)
            exponent(0, 0, [attend.step(0, j) for j in range(2)])
            attend_chunk(0, "layer one", True)
            attend_chunk(1, "layer two", True)
            with act.Fori(2, CHUNKS - 1) as c:
                attend_chunk(c, "layer two", True)
            attend_chunk(CHUNKS - 1, "layer two", False)
            for r in range(RG):
                gates(CHUNKS - 1, r)
                squash(CHUNKS - 1, r)
            normalise(2 * CHUNKS)

        @block.gpsimd
        def _(pool):
            def layer_one(c):
                for r in range(RG):
                    f = RG * c + r
                    pool.wait_ge(relu_done, f + 1)
                    if r == 0 and not (isinstance(c, int) and c == 0):
                        pool.wait_ge(dots_done, RG * c)
                        pool.wait_ge(nodes_done, c)
                    pool.wait_ge(x_in, 16 * QUADS * CHUNKS)
                    pool.tensor_tensor(val[:, r, :], relu_sb[:, r % 2, :],
                                       nodes[:, bass.ds(f, 1), :].rearrange("p o d -> p (o d)"),
                                       ALU.add).then_inc(sum_done, 1)
                pool.wait_ge(norm_done, c + 1)
                rows = nodes[:].rearrange("p (c r) d -> p c (r d)", r=RG)[:, bass.ds(c, 1), :]
                pool.tensor_copy(rows.rearrange("p o n -> p (o n)"),
                                 val[:].rearrange("p r d -> p (r d)")).then_inc(nodes_done, 1)

            def degree_chunk(s, it):
                for k in range(TILES):
                    if SUMMED_BY[s.q][k] == "P":
                        pool.wait_ge(raw_full[k % SLOTS], 64 * s.arrivals(it, k))
                        rows = raw_t[k % SLOTS].rearrange("p (g j) -> p g j", g=BLOCKS)
                        n = P // 2
                        pool.tensor_tensor(halved, rows[:, :, 0:n], rows[:, :, n:P], ALU.add).then_inc(read_out[k % SLOTS], reads(s, k))
                        pool.drain()
                        while n > 2:
                            n //= 2
                            pool.tensor_tensor(halved[:, :, 0:n], halved[:, :, 0:n], halved[:, :, n:2 * n], ALU.add)
                            pool.drain()
                        pool.wait_ge(deg_read, 2 * s.q + it)
                        pool.tensor_tensor(deg_part[:, :, k], halved[:, :, 0], halved[:, :, 1], ALU.add).then_inc(pool_sums, 1)
                        pool.drain()

            pool.wait_ge(setup, 1)
            degree_chunk(degree[1], 0)
            degree_chunk(degree[1], 1)
            for s in degree[2:]:
                with pool.Fori(0, 2) as it:
                    degree_chunk(s, it)

            layer_one(0)
            with pool.Fori(1, CHUNKS) as c:
                layer_one(c)

            def layer_two(c):
                for r in range(RG):
                    f = RG * c + r
                    pool.wait_ge(squashed, f + 1)
                    if r == 0:
                        if isinstance(c, int) and c == 0:
                            pool.wait_ge(dots_done, RG * CHUNKS)
                            pool.wait_ge(nodes_done, CHUNKS)
                        else:
                            pool.wait_ge(stored, 16 * QUADS * c)
                    pool.tensor_tensor(val[:, r, :], zed[:, r % 2, :],
                                       nodes[:, bass.ds(f, 1), :].rearrange("p o d -> p (o d)"),
                                       ALU.add).then_inc(sum_done, 1)

            layer_two(0)
            with pool.Fori(1, CHUNKS) as c:
                layer_two(c)


N_CONSTS = 16 * (8 + 2 * 3)
N_LATE = 16 * (3 + 2 * 2)

_INS = ['x', 'adj', 'L0_gnn_weight', 'L1_gnn_W_sa', 'L1_gnn_a_sa', 'L1_gnn_W_gcnb', 'L1_gnn_b_gcnb',
        'L1_gnn_Wa', 'L1_gnn_ba', 'L1_gnn_Wb', 'L1_gnn_bb']


def kernel(**inputs):
    import numpy as np
    import concourse.bacc as bacc
    from concourse.bass_utils import run_bass_kernel_spmd as run

    nc = bacc.Bacc("TRN2", target_bir_lowering=False, num_devices=1)
    arrays = {name: np.ascontiguousarray(inputs[name]) for name in _INS}
    place = np.arange(P)
    arrays["eye"] = np.eye(P, dtype=np.float32)
    arrays["fold"] = (place[:, None] % QP == place[None, :] % QP).astype(np.float32)
    args = [nc.dram_tensor(f"in_{n}", a.shape, mybir.dt.from_np(a.dtype), kind="ExternalInput").ap()
            for n, a in arrays.items()]
    out = nc.dram_tensor("out_0", arrays["x"].shape, F32, kind="ExternalOutput").ap()
    two_layers(nc, *args, out)
    r = run(nc, [{f"in_{n}": a for n, a in arrays.items()}], core_ids=[0])
    return r.results[0]["out_0"]
```

```python
from contextlib import ExitStack

import concourse.bass as bass
from concourse import mybir

ALU = mybir.AluOpType
ACT = mybir.ActivationFunctionType
AX_X = mybir.AxisListType.X
F32 = mybir.dt.float32
F32R = mybir.dt.float32r
I32 = mybir.dt.int32

P = 128
QUADS = 4
QP = P // QUADS
STEPS = 32
CHUNKS = 8
RG = STEPS // CHUNKS
COLS = RG * P
TILES = CHUNKS
BLOCKS = COLS // QP
D = 256
PAIRS = CHUNKS // 2
EPS = 1e-5
SLOPE = 0.01
RSQRT_SEED = 0x5F3759DF
NEWTON = 3
ALL_UNITS = 2 * TILES
SLOTS = 3
SLOTS_AFTER = 2
ORDER = ((0, 1, 2, 3, 4, 5, 6, 7), (0, 2, 3, 4, 1, 5, 6, 7), (0, 4, 1, 5, 2, 6, 3, 7), (0, 1, 2, 6, 3, 4, 5, 7))
BY_ACT, BY_POOL = {True: 9, False: 5}, {True: 7, False: 3}
READS = 4

LONG = dict(project=(0, 0, 1, 1), relu=(1, 1, 2, 2), residual=(2, 2, 3, 3), norm=5, turn=(6, 7, 8, 9),
            keep=(7, 8, 9, 10), dots=(7, 8, 9, 10), table=11, x1=7)
TAIL = {
    16: LONG,
    12: LONG,
    8: dict(project=(0, 0, 1, 1), relu=(0, 0, 1, 1), residual=(1, 1, 2, 2), norm=4, turn=(4, 5, 5, 6),
            keep=(5, 6, 6, 6), dots=(5, 6, 6, 6), table=7, x1=5),
    4: dict(project=(0, 0, 1, 1), relu=(0, 0, 1, 1), residual=(1, 1, 2, 2), norm=3, turn=(3, 3, 3, 3),
            keep=(3, 3, 3, 3), dots=(3, 3, 3, 3), table=3, x1=2),
}
X1_LAST = ((CHUNKS - 2, 1), (CHUNKS - 1, 8))
OUT_AT = (0, 3, 6, 9)
LOGITS, GATES, MIX, SQUASH, STATISTICS = 1, 2, 3, 4, 5


class Pass:

    def __init__(self, kind, q, tiles_loaded, tiles_used, unit0, tile0, pass0):
        self.kind, self.q = kind, q
        self.loaded, self.used = tiles_loaded, tiles_used
        self.units = 2 * len(tiles_used)
        self.places = [k for k, t in enumerate(tiles_loaded) if t in tiles_used]
        self.slots = SLOTS if kind == "degree" else SLOTS_AFTER
        self.unit0, self.tile0, self.pass0 = unit0, tile0, pass0

    def unit(self, it, u):
        return self.unit0 + it * self.units + u

    def tile(self, it, k):
        return self.tile0 + it * len(self.loaded) + k

    def arrivals(self, it, k):
        slot = k % self.slots
        per_chunk = len(range(slot, len(self.loaded), self.slots))
        if self.kind == "degree":
            return (2 * self.q + it) * per_chunk + k // self.slots + 1
        degrees = CHUNKS * len(range(slot, TILES, SLOTS))
        return degrees + (self.tile0 - TILES * CHUNKS) // self.slots + it * per_chunk + k // self.slots + 1

    def step(self, u, j):
        return 4 * self.used[u // 2] + 2 * (u % 2) + j


def plan():
    unit = tile = done = 0
    degree, final = [], []
    for q in range(PAIRS):
        s = Pass("degree", q, list(ORDER[q]), list(range(2 * q)), unit, tile, done)
        degree.append(s)
        unit, tile, done = unit + 2 * s.units, tile + 2 * TILES, done + 2 * (q > 0)
    for q in range(PAIRS):
        left = list(range(2 * q, TILES))
        s = Pass("final", q, left, left, unit, tile, done)
        final.append(s)
        unit, tile, done = unit + 2 * s.units, tile + 2 * len(left), done + 2
    attend = Pass("attend", 0, list(range(TILES)), list(range(TILES)), unit, tile, done)
    return degree, final, attend


def two_layers(nc, x, adj, w0, w_sa, a_sa, w_gc, b_gc, wa, ba, wb, bb, eye, fold, out):
    degree, final, attend = plan()
    LAYER1_PASSES = final[0].pass0

    with ExitStack() as ctx:
        def sb(name, shape, dt=F32):
            return ctx.enter_context(nc.sbuf_tensor(name, shape, dt))

        def psum(name):
            return ctx.enter_context(nc.psum_tensor(name, [P, 512], F32))

        def sem(name):
            return ctx.enter_context(nc.semaphore(name))

        nodes = sb("nodes", [P, STEPS, D])
        sta_hi = sb("sta_hi", [P, STEPS, D], F32R)
        sta_lo = sb("sta_lo", [P, STEPS, D], F32R)
        raw = sb("raw", [P, 2 * BLOCKS * P + P])
        adjt = sb("adjt", [P, 2, 2, COLS])
        adj_hi = sb("adj_hi", [P, 2, 2, COLS], F32R)
        adj_lo = sb("adj_lo", [P, 2, 2, COLS], F32R)
        e_hi = sb("e_hi", [P, 2, 2, COLS], F32R)
        e_lo = sb("e_lo", [P, 2, 2, COLS], F32R)
        room = sb("room", [P, CHUNKS, 2 * COLS])
        agg = sb("agg", [P, 2, COLS])
        eagg = sb("eagg", [P, 2, COLS])
        w0_sb = eagg[:, 0, :].rearrange("p (h n) -> p h n", h=2)
        a_row = eagg[:, 1, :].rearrange("p (h n) -> p h n", h=2)
        row_s = agg[:, 0, 0:D]
        wsa = sb("wsa", [P, 2, D + 1])
        sl_chunk = room[:, 4, COLS:2 * COLS]
        bias_g = room[:, 5, COLS:COLS + D]
        row_g = room[:, 5, COLS + D:COLS + 2 * D]
        wgc = room[:, 6:8, COLS:COLS + D + 2]
        row_gates = sb("row_gates", [P, 2])
        w4 = sb("w4", [P, 2, 4])
        wl_rep = sb("wl_rep", [P, 2, P])
        fold_sb = sb("fold_sb", [P, P])
        eye_sb = sb("eye_sb", [P, P])
        pick = sb("pick", [P, 3, P])
        bias_ab = sb("bias_ab", [P, 2])
        dinv = sb("dinv", [P, STEPS])
        degp1 = sb("degp1", [P, 8])
        seed = sb("seed", [P, 8], I32)
        tmp_d = sb("tmp_d", [P, 8])
        dinv_c = sb("dinv_c", [P, RG])
        relu_sb = sb("relu_sb", [P, 2, D])
        val = sb("val", [P, RG, D])
        deg_part = val[:, 0, 0:BLOCKS * TILES].rearrange("p (g t) -> p g t", g=BLOCKS)
        deg_sum = val[:, 1, 0:2 * BLOCKS].rearrange("p (i g) -> p i g", i=2)
        stats = sb("stats", [P, RG, 6])
        mv = sb("mv", [P, RG, 2])
        varc = sb("varc", [P, RG])
        rstd = sb("rstd", [P, RG])
        seed_v = sb("seed_v", [P, RG], I32)
        tmp_v = sb("tmp_v", [P, RG])
        shift = sb("shift", [P, RG])
        x1t = sb("x1t", [P, 2, 2, P])
        table = sb("table", [P, 4, STEPS])
        sl_scaled = sb("sl_scaled", [P, STEPS])
        tab_c = sb("tab_c", [P, RG, 3])
        gate = sb("gate", [P, RG, 7])
        mix = relu_sb
        zed = x1t[:].rearrange("p b h k -> p b (h k)")

        acc = [psum("acc_t0"), psum("acc_t1"), psum("acc_u0"), psum("acc_u1")]
        bank = [psum("bank4"), psum("bank5"), psum("bank6"), psum("bank7")]
        turned = [bank[0], bank[1]]

        raw_full = [sem(f"raw_full{b}") for b in range(SLOTS)]
        read_out = [sem(f"read_out{b}") for b in range(SLOTS)]
        pool_sums = sem("pool_sums")
        deg_read = sem("deg_read")
        consts, x_in, late_in = sem("consts"), sem("x_in"), sem("late_in")
        late_setup = sem("late_setup")
        setup = sem("setup")
        deg_pair = sem("deg_pair")
        deg_folded = sem("deg_folded")
        dinv_done = sem("dinv_done")
        stahi_ready = sem("stahi_ready")
        sta_ready = sem("sta_ready")
        x1hi_ready = sem("x1hi_ready")
        adjt_ready = sem("adjt_ready")
        hi_ready = sem("hi_ready")
        lo_ready = sem("lo_ready")
        pe_adj = sem("pe_adj")
        half0 = sem("half0")
        kept0, kept1 = sem("kept0"), sem("kept1")
        ex_mid = sem("ex_mid")
        ex_ready = sem("ex_ready")
        e_ready = sem("e_ready")
        ehi_ready = sem("ehi_ready")
        elo_ready = sem("elo_ready")
        pe_e = sem("pe_e")
        ehalf0 = sem("ehalf0")
        ekept0, ekept1 = sem("ekept0"), sem("ekept1")
        dinvc_ready = sem("dinvc_ready")
        proj = sem("proj")
        relu_done = sem("relu_done")
        sum_done = sem("sum_done")
        seed_done = sem("seed_done")
        root_done = sem("root_done")
        norm_done = sem("norm_done")
        nodes_done = sem("nodes_done")
        xt_done = sem("xt_done")
        xt_kept = sem("xt_kept")
        dots_done = sem("dots_done")
        scores_kept = sem("scores_kept")
        table_done = sem("table_done")
        tabc_done = sem("tabc_done")
        floor_done = sem("floor_done")
        logit_done = sem("logit_done")
        gates_done = sem("gates_done")
        mixed = sem("mixed")
        mix_done = sem("mix_done")
        squashed = sem("squashed")
        stored = sem("stored")

        def exb(b):
            return room[:, 2 * b:2 * b + 2, COLS:2 * COLS]

        def eb(b):
            return exb(b)

        def steps_of(t, c):
            return t[:].rearrange("p (c r) d -> p c r d", r=RG)[:, bass.ds(c, 1)].rearrange("p o r d -> p (o r) d")

        def cols(t, r):
            return t.rearrange("p (a r k) -> p a r k", a=QUADS, r=RG)[:, :, r, :]

        def by_step(t):
            return t.rearrange("p (r a k) -> p a r k", a=QUADS, r=RG)

        def by_column(t):
            return t.rearrange("p (a r k) -> p a r k", a=QUADS, r=RG)

        def step_of(t, r):
            return t[:, r * P:(r + 1) * P]

        adj_v = adj.rearrange("(c g p) (t a j) -> a p c g t j", c=CHUNKS, p=QP, a=QUADS, t=TILES)
        x_v = x.rearrange("(c a r p) d -> a p c r d", a=QUADS, c=CHUNKS, r=RG)
        out_v = out.rearrange("(c a r p) d -> a p c r d", a=QUADS, c=CHUNKS, r=RG)
        raw_t = [raw[:, b * BLOCKS * P:(b + 1) * BLOCKS * P] for b in range(2)]
        raw_t.append(room[:, 0:2, :].rearrange("p c n -> p (c n)"))
        halved = agg[:].rearrange("p h n -> p (h n)").rearrange("p (g j) -> p g j", g=BLOCKS)

        block = ctx.enter_context(nc.Block())

        @block.sync
        def _(sp):
            late = [
                (wgc[:, :, 0:D], w_gc.rearrange("(h p) n -> p h n", h=2)),
                (row_g, w_gc[D - 1, :].partition_broadcast(P)),
                (bias_g, b_gc.partition_broadcast(P)),
            ]
            for g, w in enumerate((wa, wb)):
                w_v = w.rearrange("o (k h p) -> k h p o", k=2, h=2)
                for h in range(2):
                    late.append((wgc[:, h, D + g:D + g + 1], w_v[0, h]))

            def load_tile(s, k, chunk, after):
                t, slot = s.loaded[k], k % s.slots
                for a in range(QUADS):
                    src = adj_v[a][:, bass.ds(chunk, 1), :, t, :].rearrange("p o g j -> p (o g) j")
                    if a == 0 and after is not None:
                        sp.wait_ge(*after)
                    dst = raw_t[slot][QP * a:QP * a + QP].rearrange("p (g j) -> p g j", g=BLOCKS)
                    sp.dma_start(dst, src).then_inc(raw_full[slot], 16)

            def load_late():
                sp.wait_ge(kept1, attend.pass0)
                for dst, src in late:
                    sp.dma_start(dst, src).then_inc(late_in, 16)

            def load_pass(s, it, chunk, midway=None):
                def last_reader(k):
                    if s.kind == "degree":
                        if s.q == 0 and it == 0 and k < SLOTS:
                            return None
                        return read_out[k % SLOTS], sp.snap(READS * (s.arrivals(it, k) - 1))
                    if s is final[0] and it == 0 and k < 2:
                        return read_out[k], READS * degree[PAIRS - 1].arrivals(1, TILES - SLOTS_AFTER + k)
                    return adjt_ready, sp.snap(s.unit(it, 0) + 2 * (k - 1))

                after = [last_reader(k) for k in range(len(s.loaded))]
                for k in range(len(s.loaded)):
                    if k == 2 and midway is not None:
                        midway()
                    load_tile(s, k, chunk, after[k])

            load_pass(degree[0], 0, 0)
            load_pass(degree[0], 1, 1)
            for s in degree[1:]:
                with sp.Fori(0, 2) as it:
                    load_pass(s, it, 2 * s.q + it)
            load_pass(final[0], 0, 0)
            load_pass(final[0], 1, 1)
            for s in final[1:]:
                with sp.Fori(0, 2) as it:
                    load_pass(s, it, 2 * s.q + it)

            def store(c, n_norm):
                for a in range(QUADS):
                    dst = out_v[a][:, bass.ds(c, 1), :, :].rearrange("p o r d -> p (o r) d")
                    if a == 0:
                        sp.wait_ge(norm_done, n_norm)
                    sp.dma_start(dst, val[QP * a:QP * a + QP]).then_inc(stored, 16)

            load_pass(attend, 0, 0, midway=load_late)
            load_pass(attend, 1, 1)
            with sp.Fori(2, CHUNKS) as c:
                n_norm = sp.snap(CHUNKS + c - 1)
                load_pass(attend, c, c, midway=lambda: store(c - 2, n_norm))
            store(CHUNKS - 2, 2 * CHUNKS - 1)
            store(CHUNKS - 1, 2 * CHUNKS)
            sp.wait_ge(stored, 16 * QUADS * CHUNKS)

        @block.tensor
        def _(pe):
            def product(s, u, it, moving_hi, moving_lo, banks, b, first_sem, done_sem):
                last_unit = u == s.units - 1
                for h in range(2):
                    if u == 0:
                        p = s.pass0 + it
                        if done_sem is pe_e:
                            p = it
                        if not (isinstance(p, int) and p == 0):
                            pe.wait_ge([kept0, kept1][h] if done_sem is pe_adj else [ekept0, ekept1][h], p)
                    for j in range(2):
                        st = s.step(u, j)
                        parts = ((sta_hi, moving_hi), (sta_lo, moving_hi), (sta_hi, moving_lo))
                        for k, (sta, mov) in enumerate(parts):
                            mm = pe.matmul(banks[h][:], sta[:, st, h * P:(h + 1) * P], mov[:, b, j, :],
                                           start=(u == 0 and j == 0 and k == 0),
                                           stop=(last_unit and j == 1 and k == 2))
                    if h == 0 and last_unit:
                        mm.then_inc(first_sem, 1)
                mm.then_inc(done_sem, 1)

            def adj_unit(s, it, u):
                pe.wait_ge(lo_ready, s.unit(it, u) + 1)
                product(s, u, it, adj_hi, adj_lo, acc[0:2], u % 2, half0, pe_adj)

            def project(c, r):
                f = RG * c + r
                if r == 0:
                    pe.wait_ge(kept0, LAYER1_PASSES + c + 1)
                    pe.wait_ge(kept1, LAYER1_PASSES + c + 1)
                if not (isinstance(f, int) and f < 2):
                    pe.wait_ge(relu_done, f - 1)
                for h in range(2):
                    mm = pe.matmul(bank[r % 2][:, 0:D], step_of(agg[:, h, :], r), w0_sb[:, h, :],
                                   start=(h == 0), stop=(h == 1))
                mm.then_inc(proj, 1)

            def turn(c, r):
                f = RG * c + r
                if r == 0:
                    pe.wait_ge(norm_done, c + 1)
                    if not isinstance(c, int) or c > 0:
                        pe.wait_ge(scores_kept, c)
                        pe.wait_ge(table_done, c)
                if not (isinstance(f, int) and f < 2):
                    pe.wait_ge(xt_kept, f - 1)
                for h in range(2):
                    mm = pe.transpose(turned[r % 2][:, h * P:(h + 1) * P], val[:, r, h * P:(h + 1) * P], eye_sb[:])
                mm.then_inc(xt_done, 1)

            def dots(c, r):
                pe.wait_ge(xt_kept, RG * c + r + 1)
                for h in range(2):
                    pe.matmul(cols(bank[3][:], r), wl_rep[:, h, :], x1t[:, r % 2, h, :],
                              start=(h == 0), stop=(h == 1))
                for h in range(2):
                    mm = pe.matmul(bank[2][:, D + 4 * r:D + 4 * r + 4], x1t[:, r % 2, h, :], w4[:, h, :],
                                   start=(h == 0), stop=(h == 1))
                mm.then_inc(dots_done, 1)

            def tail_one(c, units, u):
                at = TAIL[units]
                for r in range(RG):
                    if at["project"][r] == u:
                        project(c, r)
                for r in range(RG + 1):
                    if r < RG and at["turn"][r] == u:
                        turn(c, r)
                    if r and at["dots"][r - 1] == u:
                        dots(c, r - 1)

            def project_out(c, r):
                f = RG * c + r
                if r == 0:
                    pe.wait_ge(kept0, attend.pass0 + c + 1)
                    pe.wait_ge(kept1, attend.pass0 + c + 1)
                    pe.wait_ge(ekept0, c + 1)
                    pe.wait_ge(ekept1, c + 1)
                if isinstance(f, int) and f < 2:
                    pe.wait_ge(late_setup, 1)
                    pe.wait_ge(relu_done, RG * CHUNKS)
                    pe.wait_ge(scores_kept, CHUNKS)
                    pe.wait_ge(table_done, CHUNKS)
                else:
                    pe.wait_ge(mix_done, f - 1)
                for src, w, n, b in ((agg, wgc, D + 2, r % 2), (eagg, wsa, D + 1, 2 + r % 2)):
                    for h in range(2):
                        mm = pe.matmul(bank[b][:, 0:n], step_of(src[:, h, :], r), w[:, h, :],
                                       start=(h == 0), stop=(h == 1))
                mm.then_inc(proj, 1)

            def degree_chunk(s, it):
                for u in range(s.units):
                    if u == 4 * (s.q - 1):
                        pe.wait_ge(sta_ready, s.q)
                    adj_unit(s, it, u)

            for s in degree:
                if s.q == 1:
                    degree_chunk(s, 0)
                    degree_chunk(s, 1)
                elif s.units:
                    with pe.Fori(0, 2) as it:
                        degree_chunk(s, it)
                pe.wait_ge(deg_pair, s.q + 1)
                if s.q == 0:
                    pe.wait_ge(consts, N_CONSTS)
                pe.matmul(bank[3][:, 0:2 * BLOCKS], fold_sb[:], deg_sum.rearrange("p i g -> p (i g)"),
                          start=True, stop=True).then_inc(deg_folded, 1)

            def final_chunk(s, it, prev):
                for u in range(s.units):
                    adj_unit(s, it, u)
                    if prev is not None:
                        tail_one(prev, s.units, u)

            pe.wait_ge(sta_ready, PAIRS)
            pe.wait_ge(setup, 1)
            final_chunk(final[0], 0, None)
            final_chunk(final[0], 1, 0)
            for s in final[1:3]:
                with pe.Fori(0, 2) as it:
                    final_chunk(s, it, 2 * s.q + it - 1)
            final_chunk(final[3], 0, 5)
            final_chunk(final[3], 1, 6)

            def attend_chunk(c, tail):
                for u in range(attend.units):
                    if isinstance(c, int) and c == 0 and u % 2 == 0:
                        pe.wait_ge(sta_ready, PAIRS + u // 2 + 1)
                    adj_unit(attend, c, u)
                    pe.wait_ge(elo_ready, ALL_UNITS * c + u + 1)
                    product(attend, u, c, e_hi, e_lo, acc[2:4], u % 2, ehalf0, pe_e)
                    if tail == "layer one":
                        tail_one(CHUNKS - 1, attend.units, u)
                    for r in range(RG):
                        if tail == "layer two" and OUT_AT[r] == u:
                            project_out(c - 1, r)

            attend_chunk(0, "layer one")
            attend_chunk(1, "layer two")
            with pe.Fori(2, CHUNKS) as c:
                attend_chunk(c, "layer two")
            for r in range(RG):
                project_out(CHUNKS - 1, r)

        @block.vector
        def _(dve):
            def settle(dst, src, op_seed, a, b):
                dve.tensor_scalar(a, src, 1, None, ALU.logical_shift_right)
                dve.drain()
                dve.tensor_scalar(b, a, -1.0, float(RSQRT_SEED), ALU.mult, ALU.add)

            def transpose_unit(s, it, u, diagonal):
                n = s.unit(it, u)
                k = s.places[u // 2] if u < s.units else len(s.loaded)
                again = s.kind == "degree" and k == TILES
                slot = 0 if again else k % s.slots
                arrived = s.arrivals(it, TILES - SLOTS + 1) + 1 if again else s.arrivals(it, k)
                if u % 2 == 0:
                    dve.wait_ge(raw_full[slot], 64 * arrived)
                if diagonal is not None:
                    for a in range(QUADS):
                        at = slot * BLOCKS * P + RG * a * P
                        d = raw[QP * a:QP * a + QP, at:at + RG * (P + QP)].rearrange(
                            "p (r j) -> p r j", r=RG)[:, :, 0:QP]
                        i = pick[QP * a:QP * a + QP, bass.ds(diagonal, 1), :].rearrange(
                            "p o (r j) -> p (o r) j", r=RG)
                        dve.tensor_tensor(d, d, i, ALU.add)
                    dve.drain()
                if not (isinstance(n, int) and n < 2):
                    dve.wait_ge(hi_ready, n - 1)
                    dve.wait_ge(lo_ready, n - 1)
                if s.kind == "attend":
                    m = ALL_UNITS * it + u
                    if not (isinstance(m, int) and m < 2):
                        dve.wait_ge(e_ready, m - 1)
                src = raw_t[slot].rearrange("p (g s j) -> p s g j", g=BLOCKS, s=RG)[:, 2 * (u % 2):2 * (u % 2) + 2]
                dve.transpose(adjt[:, u % 2].rearrange("p s (g i) -> p s g i", i=QP), src).then_inc(adjt_ready, 1)
                if s.kind == "degree" and u % 2:
                    dve.drain()
                    dve.nop().then_inc(read_out[slot], READS - 2)

            def low_part(s, it, u):
                n = s.unit(it, u)
                dve.wait_ge(hi_ready, n + 1)
                if not (isinstance(n, int) and n < 2):
                    dve.wait_ge(pe_adj, n - 1)
                b = u % 2
                dve.tensor_tensor(adj_lo[:, b], adjt[:, b], adj_hi[:, b].bitcast(F32), ALU.subtract).then_inc(lo_ready, 1)

            def masked(c, u):
                n, b = ALL_UNITS * c + u, u % 2
                dve.wait_ge(ex_ready, 2 * (n + 1))
                dve.wait_ge(adjt_ready, attend.unit(c, u) + 1)
                if not (isinstance(n, int) and n < 2):
                    dve.wait_ge(ehi_ready, n - 1)
                    dve.wait_ge(elo_ready, n - 1)
                dve.scalar_tensor_tensor(out=eb(b), in0=adjt[:, b], scalar=0.0, in1=exb(b),
                                         op0=ALU.not_equal, op1=ALU.mult).then_inc(e_ready, 1)

            def e_low(c, u):
                n, b = ALL_UNITS * c + u, u % 2
                dve.wait_ge(ehi_ready, n + 1)
                if not (isinstance(n, int) and n < 2):
                    dve.wait_ge(pe_e, n - 1)
                dve.tensor_tensor(e_lo[:, b], eb(b), e_hi[:, b].bitcast(F32), ALU.subtract).then_inc(elo_ready, 1)

            def newton(v, y, t):
                for _ in range(NEWTON):
                    dve.scalar_tensor_tensor(out=t, in0=y, scalar=-0.5, in1=y, op0=ALU.mult, op1=ALU.mult)
                    dve.drain()
                    dve.tensor_tensor(t, t, v, ALU.mult)
                    dve.drain()
                    dve.scalar_tensor_tensor(out=y, in0=t, scalar=1.5, in1=y, op0=ALU.add, op1=ALU.mult)
                    dve.drain()

            def degree_chunk(s, it, head, more):
                for k in range(TILES):
                    if k in s.places:
                        v = 2 * s.places.index(k)
                        if k or head:
                            transpose_unit(s, it, v, None)
                            transpose_unit(s, it, v + 1, None)
                            low_part(s, it, v)
                            low_part(s, it, v + 1)
                    else:
                        mine = slice(BY_ACT[False] + BY_POOL[False] if s.q else 0, BLOCKS)
                        dve.wait_ge(raw_full[k % SLOTS], 64 * s.arrivals(it, k))
                        dve.tensor_reduce(deg_part[:, mine, k], raw_t[k % SLOTS].rearrange("p (g j) -> p g j", g=BLOCKS)[:, mine],
                                          AX_X, ALU.add).then_inc(read_out[k % SLOTS], READS - 2 if s.q else READS)
                for k in range(TILES - SLOTS, TILES):
                    dve.wait_ge(read_out[k % SLOTS], READS * s.arrivals(it, k))
                if s.q:
                    dve.wait_ge(pool_sums, TILES * (2 * (s.q - 1) + it + 1))
                dve.wait_ge(consts, N_CONSTS)
                dve.tensor_reduce(deg_sum[:, bass.ds(it, 1), :].rearrange("p o g -> p (o g)"), deg_part,
                                  AX_X, ALU.add).then_inc(deg_read, 1)
                dve.drain()
                if more:
                    transpose_unit(s, it, s.units, None)
                    transpose_unit(s, it, s.units + 1, None)
                if s.units:
                    dve.wait_ge(half0, s.pass0 + it + 1)
                    dve.wait_ge(consts, N_CONSTS)
                    kept = room[:, bass.ds(2 * s.q + it, 1), :].rearrange("p o n -> p (o n)")
                    dve.tensor_copy(kept[:, 0:COLS], acc[0][:]).then_inc(kept0, 1)
                    dve.wait_ge(pe_adj, s.unit(it, s.units))
                    dve.wait_ge(consts, N_CONSTS)
                    dve.tensor_copy(kept[:, COLS:2 * COLS], acc[1][:]).then_inc(kept1, 1)
                if more:
                    low_part(s, it, s.units)
                    low_part(s, it, s.units + 1)

            for s in degree:
                if s.q == 0:
                    with dve.Fori(0, 2) as it:
                        degree_chunk(s, it, False, False)
                elif s.q == 2:
                    with dve.Fori(0, 2) as it:
                        degree_chunk(s, it, False, True)
                else:
                    degree_chunk(s, 0, s.q == 1, True)
                    degree_chunk(s, 1, False, s.q == 1)
                dve.drain()
                dve.nop().then_inc(deg_pair, 1)
                if s.q == PAIRS - 1:
                    transpose_unit(final[0], 0, 0, 0)
                    transpose_unit(final[0], 0, 1, None)
                    low_part(final[0], 0, 0)
                dve.wait_ge(deg_folded, s.q + 1)
                for a in range(QUADS):
                    rows = slice(QP * a, QP * a + QP)
                    dve.tensor_scalar(degp1[rows].rearrange("p (i r) -> p i r", i=2),
                                      bank[3][rows, 0:2 * BLOCKS].rearrange("p (i g) -> p i g", i=2)[:, :, RG * a:RG * a + RG],
                                      1.0, None, ALU.add)
                dve.drain()
                dv = dinv[:, 8 * s.q:8 * s.q + 8]
                settle(dv, degp1[:].bitcast(I32), RSQRT_SEED, seed[:], dv.bitcast(I32))
                dve.drain()
                newton(degp1[:], dv, tmp_d[:])
                dve.wait_ge(x_in, 16 * QUADS * CHUNKS)
                dve.nop().then_inc(dinv_done, 1)
                for st in range(8 * s.q, 8 * s.q + 8):
                    dve.wait_ge(stahi_ready, st + 1)
                    ins = dve.scalar_tensor_tensor(out=sta_lo[:, st, :], in0=nodes[:, st, :], scalar=dinv[:, st:st + 1],
                                                   in1=sta_hi[:, st, :].bitcast(F32), op0=ALU.mult, op1=ALU.subtract)
                ins.then_inc(sta_ready, 1)
                if s.q == 0:
                    dve.tensor_copy(pick[:, 0, :], fold_sb[:])
                    dve.memset(pick[:, 1, :], 0.0)
                    dve.tensor_copy(pick[:, 2, :], fold_sb[:])
                    for h in range(2):
                        for side, col in ((1, 0), (0, 1)):
                            dve.tensor_tensor_reduce(out=relu_sb[:, 0, :], in0=wsa[:, h, 0:D], in1=a_row[:, side, :],
                                                     scale=1.0, scalar=0.0, op0=ALU.mult, op1=ALU.add,
                                                     accum_out=w4[:, h, col:col + 1])
                            dve.drain()
                        dve.tensor_scalar(wl_rep[:, h, :], fold_sb[:], 0.0, w4[:, h, 1:2], ALU.mult, ALU.add)
                        dve.tensor_tensor(wsa[:, h, 0:D], wsa[:, h, 0:D], row_s, ALU.subtract)
                    dve.memset(wsa[:, 0, D:D + 1], 0.0)
                    dve.tensor_copy(wsa[:, 1, D:D + 1], eye_sb[:, P - 1:P])
                    dve.drain()
                    dve.nop().then_inc(setup, 1)

            def chunk_statistics():
                dve.drain()
                dve.tensor_scalar(varc[:], mv[:, :, 1], EPS, None, ALU.add)
                dve.drain()
                settle(rstd, varc[:].bitcast(I32), RSQRT_SEED, seed_v[:], rstd[:].bitcast(I32))
                dve.drain()
                dve.nop().then_inc(seed_done, 1)

            def row_statistics(f, r):
                dve.wait_ge(sum_done, f + 1)
                dve.bn_stats(stats[:, r, :], val[:, r, :])
                dve.drain()
                dve.bn_aggr(mv[:, r, :], stats[:, r, :])

            def chunk_dinv(c):
                if not (isinstance(c, int) and c == 0):
                    dve.wait_ge(relu_done, RG * c)
                dve.tensor_copy(dinv_c[:], dinv[:, bass.ds(RG * c, RG)]).then_inc(dinvc_ready, 1)

            def residual(c, r):
                if r == 0 and not (isinstance(c, int) and c == 0):
                    dve.wait_ge(norm_done, c)
                row_statistics(RG * c + r, r)
                if r == RG - 1:
                    chunk_statistics()

            def keep_table(c):
                dve.wait_ge(dots_done, RG * c + RG)
                dve.wait_ge(setup, 1)
                dots = bank[2][:, D:D + 4 * RG].rearrange("p (r k) -> p k r", r=RG)
                dve.tensor_copy(table[:, :, bass.ds(RG * c, RG)], dots)
                dve.tensor_scalar(sl_scaled[:, bass.ds(RG * c, RG)], dots[:, 0, :], -SLOPE, None, ALU.mult).then_inc(table_done, 1)

            def x1_low(c, unused_from):
                dve.wait_ge(x1hi_ready, c + 1)
                dve.wait_ge(pe_adj, unused_from)
                lo = steps_of(sta_lo, c)
                dve.tensor_tensor(lo[:, :, 0:D - 1], steps_of(nodes, c)[:, :, 0:D - 1],
                                  steps_of(sta_hi, c)[:, :, 0:D - 1].bitcast(F32), ALU.subtract)
                dve.tensor_scalar(lo[:, :, D - 1], steps_of(nodes, c)[:, :, D - 1], 0.0, None,
                                  ALU.mult).then_inc(sta_ready, 1)

            def tail_one(prev, u, units):
                if TAIL[units]["project"][0] == u:
                    chunk_dinv(prev)
                for r in range(RG):
                    if TAIL[units]["residual"][r] == u:
                        residual(prev, r)

            def final_chunk(s, it, prev, next_pick):
                for u in range(s.units):
                    if u:
                        low_part(s, it, u)
                    if u + 2 < s.units:
                        transpose_unit(s, it, u + 2, 1 + it if u == 0 else None)
                    elif s.q == 3 and next_pick is None:
                        transpose_unit(attend, 0, u + 2 - s.units, None)
                    else:
                        transpose_unit(s, it, u + 2, next_pick if u + 2 == s.units else None)
                    if s.q and u == TAIL[s.units]["x1"] + 1:
                        x1_low(2 * (s.q - 1) + it, s.unit0)
                    if prev is not None:
                        tail_one(prev, u, s.units)
                        if TAIL[s.units]["table"] == u and u < s.units - 1:
                            keep_table(prev)
                if s.q == 3 and next_pick is None:
                    low_part(attend, 0, 0)
                    masked(0, 0)
                else:
                    low_part(s, it, s.units)
                dve.wait_ge(half0, s.pass0 + it + 1)
                if prev is not None or s.q:
                    dve.wait_ge(proj, RG * (2 * s.q + it))
                c = 2 * s.q + it
                part = room[:, bass.ds(c, 1), :].rearrange("p o n -> p (o n)")
                if s.q:
                    dve.tensor_tensor(by_step(agg[:, 0, :]), by_column(acc[0][:]), by_column(part[:, 0:COLS]), ALU.add).then_inc(kept0, 1)
                else:
                    dve.tensor_copy(by_step(agg[:, 0, :]), by_column(acc[0][:])).then_inc(kept0, 1)
                dve.wait_ge(pe_adj, s.unit(it, s.units))
                if s.q:
                    dve.tensor_tensor(by_step(agg[:, 1, :]), by_column(acc[1][:]), by_column(part[:, COLS:2 * COLS]), ALU.add).then_inc(kept1, 1)
                else:
                    dve.tensor_copy(by_step(agg[:, 1, :]), by_column(acc[1][:])).then_inc(kept1, 1)
                if prev is not None and TAIL[s.units]["table"] == s.units - 1:
                    keep_table(prev)

            final_chunk(final[0], 0, None, 1)
            final_chunk(final[0], 1, 0, 0)
            for s in final[1:3]:
                with dve.Fori(0, 2) as it:
                    final_chunk(s, it, 2 * s.q + it - 1, 1 + it)
            final_chunk(final[3], 0, 5, 1)
            final_chunk(final[3], 1, 6, None)

            def gates_in(c, r):
                f = RG * c + r
                if r == 0:
                    if not (isinstance(c, int) and c == 0):
                        dve.wait_ge(gates_done, RG * c)
                    dve.tensor_tensor(tab_c[:, :, 1:3], table[:, 2:4, bass.ds(RG * c, RG)].rearrange("p k r -> p r k"),
                                      bias_ab[:].unsqueeze(1).broadcast_to((P, RG, 2)), ALU.add)
                    dve.tensor_copy(tab_c[:, :, 0], table[:, 1, bass.ds(RG * c, RG)])
                    dve.drain()
                    dve.nop().then_inc(tabc_done, 1)
                dve.wait_ge(proj, RG * (CHUNKS + c) + r + 1)
                dve.tensor_tensor(gate[:, r, 0:2], bank[r % 2][:, D:D + 2], tab_c[:, r, 1:3], ALU.add).then_inc(logit_done, 1)

            def mix_in(c, r):
                f = RG * c + r
                dve.wait_ge(gates_done, f + 1)
                dve.tensor_scalar(gate[:, r, 0:2], gate[:, r, 2:4], 0.5, 0.5, ALU.mult, ALU.add)
                dve.scalar_tensor_tensor(out=gate[:, r, 4:5], in0=tab_c[:, r, 0:1], scalar=EPS,
                                         in1=bank[2 + r % 2][:, D:D + 1], op0=ALU.mult, op1=ALU.add)
                dve.drain()
                dve.reciprocal(gate[:, r, 5:6], gate[:, r, 4:5])
                dve.drain()
                dve.tensor_tensor(gate[:, r, 6:7], gate[:, r, 5:6], gate[:, r, 0:1], ALU.mult)
                if not (isinstance(f, int) and f < 2):
                    dve.wait_ge(squashed, f - 1)
                dve.tensor_tensor(mix[:, r % 2, :], bank[r % 2][:, 0:D], bias_g, ALU.add)
                dve.drain()
                dve.tensor_scalar(mix[:, r % 2, :], mix[:, r % 2, :], gate[:, r, 1:2], None, ALU.mult)
                dve.drain()
                dve.scalar_tensor_tensor(out=mix[:, r % 2, :], in0=bank[2 + r % 2][:, 0:D], scalar=gate[:, r, 6:7],
                                         in1=mix[:, r % 2, :], op0=ALU.mult, op1=ALU.add).then_inc(mix_done, 1)

            def norm_in(c, r):
                if r == 0:
                    dve.wait_ge(norm_done, CHUNKS + c)
                row_statistics(RG * (CHUNKS + c) + r, r)
                if r == RG - 1:
                    chunk_statistics()

            def attend_chunk(c, tail, more):
                for u in range(attend.units):
                    if u:
                        masked(c, u)
                        low_part(attend, c, u)
                        if u + 2 < attend.units or more:
                            transpose_unit(attend, c, u + 1 if u == 1 else u + 2, None)
                    e_low(c, u)
                    if u == 1:
                        transpose_unit(attend, c, u + 2, None)
                    if tail == "layer one":
                        tail_one(CHUNKS - 1, u, attend.units)
                        if u == TAIL[attend.units]["table"]:
                            keep_table(CHUNKS - 1)
                        for last, at in X1_LAST:
                            if u == at + 1:
                                x1_low(last, attend.unit0)
                    if tail == "layer two":
                        for r in range(RG):
                            if u == OUT_AT[r] + LOGITS:
                                gates_in(c - 1, r)
                            if u == OUT_AT[r] + MIX:
                                mix_in(c - 1, r)
                            if u == OUT_AT[r] + STATISTICS:
                                norm_in(c - 1, r)
                if more:
                    masked(c, attend.units)
                    low_part(attend, c, attend.units)
                dve.wait_ge(pe_adj, attend.unit(c, attend.units))
                dve.wait_ge(proj, RG * (CHUNKS + c))
                dve.tensor_copy(by_step(agg[:, 1, :]), by_column(acc[1][:])).then_inc(kept1, 1)
                dve.wait_ge(pe_e, ALL_UNITS * (c + 1))
                dve.tensor_copy(by_step(eagg[:, 1, :]), by_column(acc[3][:])).then_inc(ekept1, 1)

            attend_chunk(0, "layer one", True)
            dve.wait_ge(late_in, N_LATE)
            for h in range(2):
                dve.tensor_tensor(wgc[:, h, 0:D], wgc[:, h, 0:D], row_g, ALU.subtract)
                dve.tensor_tensor(wgc[:, h, D:D + 2], wgc[:, h, D:D + 2], row_gates[:], ALU.subtract)
            dve.drain()
            dve.nop().then_inc(late_setup, 1)
            attend_chunk(1, "layer two", True)
            with dve.Fori(2, CHUNKS - 1) as c:
                attend_chunk(c, "layer two", True)
            attend_chunk(CHUNKS - 1, "layer two", False)
            for r in range(RG):
                gates_in(CHUNKS - 1, r)
                mix_in(CHUNKS - 1, r)
                norm_in(CHUNKS - 1, r)

        @block.scalar
        def _(act):
            act.preload_act_table(ACT.Exp)
            with act.Fori(0, CHUNKS) as c:
                for a in range(QUADS):
                    act.dma_start(nodes[QP * a:QP * a + QP, bass.ds(RG * c, RG), :],
                                  x_v[a][:, bass.ds(c, 1)].rearrange("p o r d -> p (o r) d")).then_inc(x_in, 16)
            small = [
                (fold_sb[:], fold), (eye_sb[:], eye),
                (w0_sb, w0.rearrange("(h p) n -> p h n", h=2)),
                (wsa[:, :, 0:D], w_sa.rearrange("(h p) n -> p h n", h=2)),
                (row_s, w_sa[D - 1, :].partition_broadcast(P)),
                (a_row, a_sa.rearrange("o (h n) -> o h n", h=2)[0].partition_broadcast(P)),
                (bias_ab[:, 0:1], ba.partition_broadcast(P)),
                (bias_ab[:, 1:2], bb.partition_broadcast(P)),
            ]
            for g, w in enumerate((wa, wb)):
                w_v = w.rearrange("o (k h p) -> k h p o", k=2, h=2)
                small.append((row_gates[:, g:g + 1], w[0, D - 1:D].partition_broadcast(P)))
                for h in range(2):
                    small.append((w4[:, h, 2 + g:3 + g], w_v[1, h]))
            for dst, src in small:
                act.dma_start(dst, src).then_inc(consts, 16)

            unread = [bank[b][:, g * P:(g + 1) * P] for b in range(3) for g in range(4)]
            unread += [x1t[:, b, h, :] for b in range(2) for h in range(2)]

            def high_part(s, it, u):
                n, b = s.unit(it, u), u % 2
                act.wait_ge(adjt_ready, n + 1)
                if not (isinstance(n, int) and n < 2):
                    act.wait_ge(pe_adj, n - 1)
                act.activation(adj_hi[:, b], adjt[:, b], ACT.Copy).then_inc(hi_ready, 1)

            def degree_chunk(s, it, head, more):
                for k in range(TILES):
                    products = k in s.places
                    if products and (k or head):
                        high_part(s, it, 2 * s.places.index(k))
                        high_part(s, it, 2 * s.places.index(k) + 1)
                    act.wait_ge(deg_read, 2 * s.q + it)
                    act.wait_ge(raw_full[k % SLOTS], 64 * s.arrivals(it, k))
                    rows = raw_t[k % SLOTS].rearrange("p (g j) -> p g j", g=BLOCKS)
                    for g in range(BY_ACT[products]):
                        ins = act.activation(unread[g], rows[:, g, :], ACT.Copy, accum_out=deg_part[:, g, k:k + 1])
                    ins.then_inc(read_out[k % SLOTS], 1)
                    act.drain()
                if more:
                    high_part(s, it, s.units)
                    high_part(s, it, s.units + 1)

            act.wait_ge(x_in, 16 * QUADS * CHUNKS)
            for s in degree:
                if s.q == 2:
                    with act.Fori(0, 2) as it:
                        degree_chunk(s, it, False, True)
                elif s.q:
                    degree_chunk(s, 0, s.q == 1, True)
                    degree_chunk(s, 1, False, s.q == 1)
                if s.q == PAIRS - 1:
                    high_part(final[0], 0, 0)
                act.wait_ge(dinv_done, s.q + 1)
                for st in range(8 * s.q, 8 * s.q + 8):
                    act.activation(sta_hi[:, st, :], nodes[:, st, :], ACT.Copy,
                                   scale=dinv[:, st:st + 1]).then_inc(stahi_ready, 1)

            def relu(c, r):
                f = RG * c + r
                act.wait_ge(proj, f + 1)
                if r == 0:
                    act.wait_ge(dinvc_ready, c + 1)
                if not (isinstance(f, int) and f < 2):
                    act.wait_ge(sum_done, f - 1)
                act.activation(relu_sb[:, r % 2, :], bank[r % 2][:, 0:D], ACT.Relu,
                               scale=dinv_c[:, r:r + 1]).then_inc(relu_done, 1)

            def keep_x1t(c, r):
                f = RG * c + r
                act.wait_ge(xt_done, f + 1)
                if not (isinstance(f, int) and f < 2):
                    act.wait_ge(dots_done, f - 1)
                act.activation(x1t[:, r % 2], turned[r % 2][:, 0:D].rearrange("p (h k) -> p h k", h=2),
                               ACT.Copy).then_inc(xt_kept, 1)

            def keep_scores(c):
                act.wait_ge(dots_done, RG * c + RG)
                act.wait_ge(setup, 1)
                act.activation(room[:, bass.ds(c, 1), 0:COLS].rearrange("p o n -> p (o n)"), bank[3][:],
                               ACT.Copy).then_inc(scores_kept, 1)

            def normalise(count):
                act.wait_ge(root_done, count)
                for r in range(RG):
                    ins = act.activation(val[:, r, :], val[:, r, :], ACT.Identity, bias=shift[:, r:r + 1],
                                         scale=rstd[:, r:r + 1])
                ins.then_inc(norm_done, 1)

            def tail_one(prev, u, units):
                for r in range(RG):
                    if TAIL[units]["relu"][r] == u:
                        relu(prev, r)
                if TAIL[units]["norm"] == u:
                    normalise(prev + 1)
                    act.wait_ge(norm_done, prev + 1)
                    act.wait_ge(setup, 1)
                    rows = nodes[:].rearrange("p (c r) d -> p c (r d)", r=RG)[:, bass.ds(prev, 1), :]
                    act.activation(rows.rearrange("p o n -> p (o n)"), val[:].rearrange("p r d -> p (r d)"),
                                   ACT.Copy).then_inc(nodes_done, 1)
                for r in range(RG):
                    if TAIL[units]["keep"][r] == u:
                        keep_x1t(prev, r)
                if TAIL[units]["table"] == u:
                    keep_scores(prev)

            def x1_high(c, unused_from):
                act.wait_ge(nodes_done, c + 1)
                act.wait_ge(pe_adj, unused_from)
                hi = steps_of(sta_hi, c)
                act.activation(hi[:, :, 0:D - 1], steps_of(nodes, c)[:, :, 0:D - 1], ACT.Copy)
                act.activation(hi[:, :, D - 1], steps_of(nodes, c)[:, :, D - 1], ACT.Copy, scale=0.0,
                               bias=1.0).then_inc(x1hi_ready, 1)

            def final_chunk(s, it, prev):
                for u in range(s.units):
                    high_part(s, it, u + 1)
                    if s.q and u == TAIL[s.units]["x1"]:
                        x1_high(2 * (s.q - 1) + it, s.unit0)
                    if prev is not None:
                        tail_one(prev, u, s.units)

            final_chunk(final[0], 0, None)
            final_chunk(final[0], 1, 0)
            for s in final[1:3]:
                with act.Fori(0, 2) as it:
                    final_chunk(s, it, 2 * s.q + it - 1)
            def next_scores(c):
                act.wait_ge(scores_kept, min(c, CHUNKS) + 1 if isinstance(c, int) else c + 1)
                if not (isinstance(c, int) and c == 0):
                    act.wait_ge(ex_mid, 2 * ALL_UNITS * c)
                act.wait_ge(setup, 1)
                act.activation(sl_chunk, room[:, bass.ds(c, 1), 0:COLS].rearrange("p o n -> p (o n)"), ACT.Copy)
                act.drain()

            def exponent(n, b, steps):
                if not (isinstance(n, int) and n < 2):
                    act.wait_ge(elo_ready, n - 1)
                for j, st in enumerate(steps):
                    act.activation(exb(b)[:, j, :], sl_chunk, ACT.Relu, bias=table[:, 0, st:st + 1]).then_inc(ex_mid, 1)
                act.wait_ge(ex_mid, 2 * (n + 1))
                for j, st in enumerate(steps):
                    act.activation(exb(b)[:, j, :], exb(b)[:, j, :], ACT.Exp, bias=sl_scaled[:, st:st + 1],
                                   scale=-(1 - SLOPE)).then_inc(ex_ready, 1)

            final_chunk(final[3], 0, 5)
            act.wait_ge(kept1, LAYER1_PASSES + 2 * (PAIRS - 1))
            next_scores(0)
            exponent(0, 0, [attend.step(0, j) for j in range(2)])
            final_chunk(final[3], 1, 6)

            def e_high(c, u):
                n, b = ALL_UNITS * c + u, u % 2
                act.wait_ge(e_ready, n + 1)
                if not (isinstance(n, int) and n < 2):
                    act.wait_ge(pe_e, n - 1)
                act.activation(e_hi[:, b], eb(b), ACT.Copy).then_inc(ehi_ready, 1)

            def gates(c, r):
                f = RG * c + r
                if r == 0:
                    act.wait_ge(tabc_done, c + 1)
                    act.activation(tab_c[:, :, 0], tab_c[:, :, 0], ACT.Exp, scale=SLOPE)
                act.wait_ge(logit_done, f + 1)
                act.activation(gate[:, r, 2:4], gate[:, r, 0:2], ACT.Tanh, scale=0.5).then_inc(gates_done, 1)

            def squash(c, r):
                f = RG * c + r
                act.wait_ge(mix_done, f + 1)
                if not (isinstance(f, int) and f < 2):
                    act.wait_ge(sum_done, RG * CHUNKS + f - 1)
                act.activation(zed[:, r % 2, :], mix[:, r % 2, :], ACT.Tanh, scale=0.5)
                act.drain()
                act.activation(zed[:, r % 2, :], zed[:, r % 2, :], ACT.Copy, scale=0.5,
                               bias=0.5).then_inc(squashed, 1)

            def attend_chunk(c, tail, more):
                for u in range(attend.units):
                    e_high(c, u)
                    if u + 1 < attend.units:
                        exponent(ALL_UNITS * c + u + 1, (u + 1) % 2, [attend.step(u + 1, j) for j in range(2)])
                        high_part(attend, c, u + 1)
                    elif more:
                        next_scores(c + 1)
                        exponent(ALL_UNITS * (c + 1), 0, [attend.step(0, j) for j in range(2)])
                        high_part(attend, c + 1, 0)
                    if tail == "layer one":
                        tail_one(CHUNKS - 1, u, attend.units)
                        for last, at in X1_LAST:
                            if u == at:
                                x1_high(last, attend.unit0)
                    if tail == "layer two":
                        for r in range(RG):
                            if u == OUT_AT[r] + GATES:
                                gates(c - 1, r)
                            if u == OUT_AT[r] + SQUASH:
                                squash(c - 1, r)
                        if u == 0 and not (isinstance(c, int) and c == 1):
                            normalise(CHUNKS + c - 1)
                p = attend.pass0 + c + 1
                act.wait_ge(half0, p)
                act.wait_ge(proj, RG * (CHUNKS + c))
                act.activation(by_step(agg[:, 0, :]), by_column(acc[0][:]), ACT.Copy).then_inc(kept0, 1)
                act.wait_ge(ehalf0, c + 1)
                act.activation(by_step(eagg[:, 0, :]), by_column(acc[2][:]), ACT.Copy).then_inc(ekept0, 1)

            attend_chunk(0, "layer one", True)
            attend_chunk(1, "layer two", True)
            with act.Fori(2, CHUNKS - 1) as c:
                attend_chunk(c, "layer two", True)
            attend_chunk(CHUNKS - 1, "layer two", False)
            normalise(2 * CHUNKS - 1)
            for r in range(RG):
                gates(CHUNKS - 1, r)
                squash(CHUNKS - 1, r)
            normalise(2 * CHUNKS)

        @block.gpsimd
        def _(pool):
            def root(count):
                pool.wait_ge(seed_done, count)
                for _ in range(NEWTON):
                    pool.tensor_tensor(tmp_v[:], rstd[:], rstd[:], ALU.mult)
                    pool.drain()
                    pool.tensor_tensor(tmp_v[:], tmp_v[:], varc[:], ALU.mult)
                    pool.drain()
                    pool.tensor_scalar(tmp_v[:], tmp_v[:], -0.5, 1.5, ALU.mult, ALU.add)
                    pool.drain()
                    pool.tensor_tensor(rstd[:], rstd[:], tmp_v[:], ALU.mult)
                    pool.drain()
                pool.tensor_tensor(shift[:], mv[:, :, 0], rstd[:], ALU.mult)
                pool.drain()
                pool.tensor_scalar(shift[:], shift[:], -1.0, None, ALU.mult).then_inc(root_done, 1)

            def layer_one(c):
                for r in range(RG):
                    f = RG * c + r
                    pool.wait_ge(relu_done, f + 1)
                    if r == 0 and not (isinstance(c, int) and c == 0):
                        pool.wait_ge(dots_done, RG * c)
                        pool.wait_ge(nodes_done, c)
                    pool.wait_ge(x_in, 16 * QUADS * CHUNKS)
                    pool.tensor_tensor(val[:, r, :], relu_sb[:, r % 2, :],
                                       nodes[:, bass.ds(f, 1), :].rearrange("p o d -> p (o d)"),
                                       ALU.add).then_inc(sum_done, 1)
                root(c + 1)

            def degree_chunk(s, it):
                for k in range(TILES):
                    first = BY_ACT[k in s.places]
                    count = BY_POOL[k in s.places]
                    mine = slice(first, first + count)
                    pool.wait_ge(raw_full[k % SLOTS], 64 * s.arrivals(it, k))
                    rows = raw_t[k % SLOTS].rearrange("p (g j) -> p g j", g=BLOCKS)[:, mine]
                    part = halved[:, 0:count]
                    n = P // 2
                    pool.tensor_tensor(part, rows[:, :, 0:n], rows[:, :, n:P], ALU.add).then_inc(read_out[k % SLOTS], 1)
                    pool.drain()
                    while n > 2:
                        n //= 2
                        pool.tensor_tensor(part[:, :, 0:n], part[:, :, 0:n], part[:, :, n:2 * n], ALU.add)
                        pool.drain()
                    pool.wait_ge(deg_read, 2 * s.q + it)
                    pool.tensor_tensor(deg_part[:, mine, k], part[:, :, 0], part[:, :, 1], ALU.add).then_inc(pool_sums, 1)
                    pool.drain()

            pool.wait_ge(setup, 1)
            degree_chunk(degree[1], 0)
            degree_chunk(degree[1], 1)
            for s in degree[2:]:
                with pool.Fori(0, 2) as it:
                    degree_chunk(s, it)

            layer_one(0)
            with pool.Fori(1, CHUNKS) as c:
                layer_one(c)

            def layer_two(c):
                for r in range(RG):
                    f = RG * c + r
                    pool.wait_ge(squashed, f + 1)
                    if r == 0:
                        if isinstance(c, int) and c == 0:
                            pool.wait_ge(dots_done, RG * CHUNKS)
                            pool.wait_ge(nodes_done, CHUNKS)
                        else:
                            pool.wait_ge(stored, 16 * QUADS * c)
                    pool.tensor_tensor(val[:, r, :], zed[:, r % 2, :],
                                       nodes[:, bass.ds(f, 1), :].rearrange("p o d -> p (o d)"),
                                       ALU.add).then_inc(sum_done, 1)
                root(CHUNKS + c + 1)

            layer_two(0)
            with pool.Fori(1, CHUNKS) as c:
                layer_two(c)


N_CONSTS = 16 * (8 + 2 * 3)
N_LATE = 16 * (3 + 2 * 2)

_INS = ['x', 'adj', 'L0_gnn_weight', 'L1_gnn_W_sa', 'L1_gnn_a_sa', 'L1_gnn_W_gcnb', 'L1_gnn_b_gcnb',
        'L1_gnn_Wa', 'L1_gnn_ba', 'L1_gnn_Wb', 'L1_gnn_bb']


def kernel(**inputs):
    import numpy as np
    import concourse.bacc as bacc
    from concourse.bass_utils import run_bass_kernel_spmd as run

    nc = bacc.Bacc("TRN2", target_bir_lowering=False, num_devices=1)
    arrays = {name: np.ascontiguousarray(inputs[name]) for name in _INS}
    place = np.arange(P)
    arrays["eye"] = np.eye(P, dtype=np.float32)
    arrays["fold"] = (place[:, None] % QP == place[None, :] % QP).astype(np.float32)
    args = [nc.dram_tensor(f"in_{n}", a.shape, mybir.dt.from_np(a.dtype), kind="ExternalInput").ap()
            for n, a in arrays.items()]
    out = nc.dram_tensor("out_0", arrays["x"].shape, F32, kind="ExternalOutput").ap()
    two_layers(nc, *args, out)
    r = run(nc, [{f"in_{n}": a for n, a in arrays.items()}], core_ids=[0])
    return r.results[0]["out_0"]
```

```python
from contextlib import ExitStack

import concourse.bass as bass
from concourse import mybir

ALU = mybir.AluOpType
ACT = mybir.ActivationFunctionType
AX_X = mybir.AxisListType.X
F32 = mybir.dt.float32
F32R = mybir.dt.float32r
I32 = mybir.dt.int32

P = 128
QUADS = 4
QP = P // QUADS
STEPS = 32
CHUNKS = 8
RG = STEPS // CHUNKS
COLS = RG * P
TILES = CHUNKS
BLOCKS = COLS // QP
D = 256
PAIRS = CHUNKS // 2
EPS = 1e-5
SLOPE = 0.01
RSQRT_SEED = 0x5F3759DF
NEWTON = 3
ALL_UNITS = 2 * TILES
SLOTS = 4
SLOTS_AFTER = 2
ORDER = ((0, 1, 2, 3, 4, 5, 6, 7), (0, 2, 3, 4, 1, 5, 6, 7), (0, 4, 1, 5, 2, 6, 3, 7), (0, 1, 2, 6, 3, 4, 5, 7))
BY_ACT, BY_POOL = {True: 9, False: 5}, {True: 7, False: 3}
READS = 4

LONG = dict(project=(0, 0, 1, 1), relu=(1, 1, 2, 2), residual=(2, 2, 3, 3), norm=5, turn=(6, 7, 8, 9),
            keep=(7, 8, 9, 10), dots=(7, 8, 9, 10), table=11, x1=7)
TAIL = {
    16: LONG,
    12: LONG,
    8: dict(project=(0, 0, 1, 1), relu=(0, 0, 1, 1), residual=(1, 1, 2, 2), norm=4, turn=(4, 5, 5, 6),
            keep=(5, 6, 6, 6), dots=(5, 6, 6, 6), table=7, x1=5),
    4: dict(project=(0, 0, 1, 1), relu=(0, 0, 1, 1), residual=(1, 1, 2, 2), norm=3, turn=(3, 3, 3, 3),
            keep=(3, 3, 3, 3), dots=(3, 3, 3, 3), table=3, x1=2),
}
X1_LAST = ((CHUNKS - 2, 1), (CHUNKS - 1, 8))
HALVES = 2
OUT_AT = (0, 8)
LOGITS, GATES, GATES_USED, MIX, SQUASH, STATISTICS = 1, 2, 3, 4, 5, 6


class Pass:

    def __init__(self, kind, q, tiles_loaded, tiles_used, unit0, tile0, pass0):
        self.kind, self.q = kind, q
        self.loaded, self.used = tiles_loaded, tiles_used
        self.units = 2 * len(tiles_used)
        self.places = [k for k, t in enumerate(tiles_loaded) if t in tiles_used]
        self.slots = SLOTS if kind == "degree" else SLOTS_AFTER
        self.unit0, self.tile0, self.pass0 = unit0, tile0, pass0

    def unit(self, it, u):
        return self.unit0 + it * self.units + u

    def tile(self, it, k):
        return self.tile0 + it * len(self.loaded) + k

    def arrivals(self, it, k):
        slot = k % self.slots
        per_chunk = len(range(slot, len(self.loaded), self.slots))
        if self.kind == "degree":
            return (2 * self.q + it) * per_chunk + k // self.slots + 1
        degrees = CHUNKS * len(range(slot, TILES, SLOTS))
        return degrees + (self.tile0 - TILES * CHUNKS) // self.slots + it * per_chunk + k // self.slots + 1

    def step(self, u, j):
        return 4 * self.used[u // 2] + 2 * (u % 2) + j


def plan():
    unit = tile = done = 0
    degree, final = [], []
    for q in range(PAIRS):
        s = Pass("degree", q, list(ORDER[q]), list(range(2 * q)), unit, tile, done)
        degree.append(s)
        unit, tile, done = unit + 2 * s.units, tile + 2 * TILES, done + 2 * (q > 0)
    for q in range(PAIRS):
        left = list(range(2 * q, TILES))
        s = Pass("final", q, left, left, unit, tile, done)
        final.append(s)
        unit, tile, done = unit + 2 * s.units, tile + 2 * len(left), done + 2
    attend = Pass("attend", 0, list(range(TILES)), list(range(TILES)), unit, tile, done)
    return degree, final, attend


def two_layers(nc, x, adj, w0, w_sa, a_sa, w_gc, b_gc, wa, ba, wb, bb, eye, fold, out):
    degree, final, attend = plan()
    LAYER1_PASSES = final[0].pass0

    with ExitStack() as ctx:
        def sb(name, shape, dt=F32):
            return ctx.enter_context(nc.sbuf_tensor(name, shape, dt))

        def psum(name):
            return ctx.enter_context(nc.psum_tensor(name, [P, 512], F32))

        def sem(name):
            return ctx.enter_context(nc.semaphore(name))

        nodes = sb("nodes", [P, STEPS, D])
        sta_hi = sb("sta_hi", [P, STEPS, D], F32R)
        sta_lo = sb("sta_lo", [P, STEPS, D], F32R)
        raw = sb("raw", [P, 2 * BLOCKS * P + P])
        adjt = sb("adjt", [P, 2, 2, COLS])
        adj_hi = sb("adj_hi", [P, 2, 2, COLS], F32R)
        adj_lo = sb("adj_lo", [P, 2, 2, COLS], F32R)
        e_hi = sb("e_hi", [P, 2, 2, COLS], F32R)
        e_lo = sb("e_lo", [P, 2, 2, COLS], F32R)
        room = sb("room", [P, CHUNKS, 2 * COLS])
        spare = sb("spare", [P, BLOCKS * P])
        agg = spare[:, 0:2 * COLS].rearrange("p (h n) -> p h n", h=2)
        relu_sb = spare[:, 2 * COLS:2 * COLS + 2 * D].rearrange("p (b n) -> p b n", b=2)
        x1t = spare[:, 2 * COLS + 2 * D:2 * COLS + 4 * D].rearrange("p (b h k) -> p b h k", b=2, h=2)
        eagg = sb("eagg", [P, 2, COLS])
        w0_sb = eagg[:, 0, :].rearrange("p (h n) -> p h n", h=2)
        a_row = eagg[:, 1, :].rearrange("p (h n) -> p h n", h=2)
        wsa = sb("wsa", [P, 2, D + 1])
        sl_chunk = room[:, 4, COLS:2 * COLS]
        bias_g = room[:, 5, COLS:COLS + D]
        row_g = room[:, 5, COLS + D:COLS + 2 * D]
        wgc = room[:, 6:8, COLS:COLS + D + 2]
        row_gates = sb("row_gates", [P, 2])
        w4 = sb("w4", [P, 2, 4])
        wl_rep = sb("wl_rep", [P, 2, P])
        fold_sb = sb("fold_sb", [P, P])
        eye_sb = sb("eye_sb", [P, P])
        pick = sb("pick", [P, 3, P])
        bias_ab = sb("bias_ab", [P, 2])
        dinv = sb("dinv", [P, STEPS])
        degp1 = sb("degp1", [P, 8])
        seed = sb("seed", [P, 8], I32)
        tmp_d = sb("tmp_d", [P, 8])
        dinv_c = sb("dinv_c", [P, RG])
        val = sb("val", [P, RG, D])
        deg_part = val[:, 0, 0:BLOCKS * TILES].rearrange("p (g t) -> p g t", g=BLOCKS)
        row_s, products = val[:, 2, :], val[:, 3, :]
        halved = val[:, 2:4, :].rearrange("p r d -> p (r d)").rearrange("p (g j) -> p g j", j=P // 2)
        deg_sum = val[:, 1, 0:2 * BLOCKS].rearrange("p (i g) -> p i g", i=2)
        stats = sb("stats", [P, RG, 6])
        mv = sb("mv", [P, RG, 2])
        varc = sb("varc", [P, RG])
        rstd = sb("rstd", [P, RG])
        seed_v = sb("seed_v", [P, RG], I32)
        tmp_v = sb("tmp_v", [P, RG])
        shift = sb("shift", [P, RG])
        table = sb("table", [P, 4, STEPS])
        sl_scaled = sb("sl_scaled", [P, STEPS])
        tab_c = sb("tab_c", [P, RG, 3])
        gate = sb("gate", [P, RG, 7])
        mix = relu_sb
        zed = x1t.rearrange("p b h k -> p b (h k)")

        acc = [psum("acc_t0"), psum("acc_t1"), psum("acc_u0"), psum("acc_u1")]
        bank = [psum("bank4"), psum("bank5"), psum("bank6"), psum("bank7")]
        turned = [bank[0], bank[1]]

        raw_full = [sem(f"raw_full{b}") for b in range(SLOTS)]
        read_out = [sem(f"read_out{b}") for b in range(SLOTS)]
        pool_sums = sem("pool_sums")
        deg_read = sem("deg_read")
        consts, late_in = sem("consts"), sem("late_in")
        x_first, x_in = sem("x_first"), sem("x_in")
        late_setup = sem("late_setup")
        setup = sem("setup")
        deg_folded = sem("deg_folded")
        dinv_done = sem("dinv_done")
        stahi_ready = sem("stahi_ready")
        sta_ready = sem("sta_ready")
        x1hi_ready = sem("x1hi_ready")
        adjt_ready = sem("adjt_ready")
        hi_ready = sem("hi_ready")
        lo_ready = sem("lo_ready")
        pe_adj = sem("pe_adj")
        half0 = sem("half0")
        kept0, kept1 = sem("kept0"), sem("kept1")
        ex_mid = sem("ex_mid")
        ex_ready = sem("ex_ready")
        e_ready = sem("e_ready")
        ehi_ready = sem("ehi_ready")
        elo_ready = sem("elo_ready")
        pe_e = sem("pe_e")
        ehalf0 = sem("ehalf0")
        ekept0, ekept1 = sem("ekept0"), sem("ekept1")
        dinvc_ready = sem("dinvc_ready")
        proj = sem("proj")
        relu_done = sem("relu_done")
        sum_done = sem("sum_done")
        seed_done = sem("seed_done")
        root_done = sem("root_done")
        norm_done = sem("norm_done")
        nodes_done = sem("nodes_done")
        xt_done = sem("xt_done")
        xt_kept = sem("xt_kept")
        dots_done = sem("dots_done")
        scores_kept = sem("scores_kept")
        table_done = sem("table_done")
        tabc_done = sem("tabc_done")
        floor_done = sem("floor_done")
        logit_done = sem("logit_done")
        gates_done = sem("gates_done")
        mixed = sem("mixed")
        mix_done = sem("mix_done")
        squashed = sem("squashed")
        stored = sem("stored")

        def exb(b):
            return room[:, 2 * b:2 * b + 2, COLS:2 * COLS]

        def eb(b):
            return exb(b)

        def steps_of(t, c):
            return t[:].rearrange("p (c r) d -> p c r d", r=RG)[:, bass.ds(c, 1)].rearrange("p o r d -> p (o r) d")

        def x_of(q):
            return (x_in, 16 * QUADS * (CHUNKS - 2)) if q else (x_first, 16 * QUADS * 2)

        def cols(t, r):
            return t.rearrange("p (a r k) -> p a r k", a=QUADS, r=RG)[:, :, r, :]

        def by_step(t):
            return t.rearrange("p (r a k) -> p a r k", a=QUADS, r=RG)

        def by_column(t):
            return t.rearrange("p (a r k) -> p a r k", a=QUADS, r=RG)

        def step_of(t, r):
            return t[:, r * P:(r + 1) * P]

        adj_v = adj.rearrange("(c g p) (t a j) -> a p c g t j", c=CHUNKS, p=QP, a=QUADS, t=TILES)
        x_v = x.rearrange("(c a r p) d -> a p c r d", a=QUADS, c=CHUNKS, r=RG)
        out_v = out.rearrange("(c a r p) d -> a p c r d", a=QUADS, c=CHUNKS, r=RG)
        raw_t = [raw[:, b * BLOCKS * P:(b + 1) * BLOCKS * P] for b in range(2)]
        raw_t.append(room[:, 0:2, :].rearrange("p c n -> p (c n)"))
        raw_t.append(spare[:])

        block = ctx.enter_context(nc.Block())

        @block.sync
        def _(sp):
            late = [
                (wgc[:, :, 0:D], w_gc.rearrange("(h p) n -> p h n", h=2)),
                (row_g, w_gc[D - 1, :].partition_broadcast(P)),
                (bias_g, b_gc.partition_broadcast(P)),
            ]
            for g, w in enumerate((wa, wb)):
                w_v = w.rearrange("o (k h p) -> k h p o", k=2, h=2)
                for h in range(2):
                    late.append((wgc[:, h, D + g:D + g + 1], w_v[0, h]))

            def load_tile(s, k, chunk, after):
                t, slot = s.loaded[k], k % s.slots
                for a in range(QUADS):
                    src = adj_v[a][:, bass.ds(chunk, 1), :, t, :].rearrange("p o g j -> p (o g) j")
                    if a == 0 and after is not None:
                        sp.wait_ge(*after)
                    dst = raw_t[slot][QP * a:QP * a + QP].rearrange("p (g j) -> p g j", g=BLOCKS)
                    sp.dma_start(dst, src).then_inc(raw_full[slot], 16)

            def load_late():
                sp.wait_ge(kept1, attend.pass0)
                for dst, src in late:
                    sp.dma_start(dst, src).then_inc(late_in, 16)

            def load_pass(s, it, chunk, midway=None):
                def last_reader(k):
                    if s.kind == "degree":
                        if s.q == 0 and it == 0 and k < SLOTS:
                            return None
                        return read_out[k % SLOTS], sp.snap(READS * (s.arrivals(it, k) - 1))
                    if s is final[0] and it == 0 and k < 2:
                        return read_out[k], READS * degree[PAIRS - 1].arrivals(1, TILES - SLOTS_AFTER + k)
                    return adjt_ready, sp.snap(s.unit(it, 0) + 2 * (k - 1))

                after = [last_reader(k) for k in range(len(s.loaded))]
                for k in range(len(s.loaded)):
                    if k == 2 and midway is not None:
                        midway()
                    load_tile(s, k, chunk, after[k])

            load_pass(degree[0], 0, 0)
            load_pass(degree[0], 1, 1)
            for s in degree[1:]:
                with sp.Fori(0, 2) as it:
                    load_pass(s, it, 2 * s.q + it)
            load_pass(final[0], 0, 0)
            load_pass(final[0], 1, 1)
            for s in final[1:]:
                with sp.Fori(0, 2) as it:
                    load_pass(s, it, 2 * s.q + it)

            def store(c, n_norm):
                for a in range(QUADS):
                    dst = out_v[a][:, bass.ds(c, 1), :, :].rearrange("p o r d -> p (o r) d")
                    if a == 0:
                        sp.wait_ge(norm_done, n_norm)
                    sp.dma_start(dst, val[QP * a:QP * a + QP]).then_inc(stored, 16)

            load_pass(attend, 0, 0, midway=load_late)
            load_pass(attend, 1, 1)
            with sp.Fori(2, CHUNKS) as c:
                n_norm = sp.snap(CHUNKS + c - 1)
                load_pass(attend, c, c, midway=lambda: store(c - 2, n_norm))
            store(CHUNKS - 2, 2 * CHUNKS - 1)
            store(CHUNKS - 1, 2 * CHUNKS)
            sp.wait_ge(stored, 16 * QUADS * CHUNKS)

        @block.tensor
        def _(pe):
            def product(s, u, it, moving_hi, moving_lo, banks, b, first_sem, done_sem):
                last_unit = u == s.units - 1
                for h in range(2):
                    if u == 0:
                        p = s.pass0 + it
                        if done_sem is pe_e:
                            p = it
                        if not (isinstance(p, int) and p == 0):
                            pe.wait_ge([kept0, kept1][h] if done_sem is pe_adj else [ekept0, ekept1][h], p)
                    for j in range(2):
                        st = s.step(u, j)
                        parts = ((sta_hi, moving_hi), (sta_lo, moving_hi), (sta_hi, moving_lo))
                        for k, (sta, mov) in enumerate(parts):
                            mm = pe.matmul(banks[h][:], sta[:, st, h * P:(h + 1) * P], mov[:, b, j, :],
                                           start=(u == 0 and j == 0 and k == 0),
                                           stop=(last_unit and j == 1 and k == 2))
                    if h == 0 and last_unit:
                        mm.then_inc(first_sem, 1)
                mm.then_inc(done_sem, 1)

            def adj_unit(s, it, u):
                pe.wait_ge(lo_ready, s.unit(it, u) + 1)
                product(s, u, it, adj_hi, adj_lo, acc[0:2], u % 2, half0, pe_adj)

            def project(c, r):
                f = RG * c + r
                if r == 0:
                    pe.wait_ge(kept0, LAYER1_PASSES + c + 1)
                    pe.wait_ge(kept1, LAYER1_PASSES + c + 1)
                if not (isinstance(f, int) and f < 2):
                    pe.wait_ge(relu_done, f - 1)
                for h in range(2):
                    mm = pe.matmul(bank[r % 2][:, 0:D], step_of(agg[:, h, :], r), w0_sb[:, h, :],
                                   start=(h == 0), stop=(h == 1))
                mm.then_inc(proj, 1)

            def turn(c, r):
                f = RG * c + r
                if r == 0:
                    pe.wait_ge(norm_done, c + 1)
                    if not isinstance(c, int) or c > 0:
                        pe.wait_ge(scores_kept, c)
                        pe.wait_ge(table_done, c)
                if not (isinstance(f, int) and f < 2):
                    pe.wait_ge(xt_kept, f - 1)
                for h in range(2):
                    mm = pe.transpose(turned[r % 2][:, h * P:(h + 1) * P], val[:, r, h * P:(h + 1) * P], eye_sb[:])
                mm.then_inc(xt_done, 1)

            def dots(c, r):
                pe.wait_ge(xt_kept, RG * c + r + 1)
                for h in range(2):
                    pe.matmul(cols(bank[3][:], r), wl_rep[:, h, :], x1t[:, r % 2, h, :],
                              start=(h == 0), stop=(h == 1))
                for h in range(2):
                    mm = pe.matmul(bank[2][:, D + 4 * r:D + 4 * r + 4], x1t[:, r % 2, h, :], w4[:, h, :],
                                   start=(h == 0), stop=(h == 1))
                mm.then_inc(dots_done, 1)

            def tail_one(c, units, u):
                at = TAIL[units]
                for r in range(RG):
                    if at["project"][r] == u:
                        project(c, r)
                for r in range(RG + 1):
                    if r < RG and at["turn"][r] == u:
                        turn(c, r)
                    if r and at["dots"][r - 1] == u:
                        dots(c, r - 1)

            def project_out(c, g):
                f = HALVES * c + g
                if g == 0:
                    pe.wait_ge(kept0, attend.pass0 + c + 1)
                    pe.wait_ge(kept1, attend.pass0 + c + 1)
                    pe.wait_ge(ekept0, c + 1)
                    pe.wait_ge(ekept1, c + 1)
                if isinstance(f, int) and f == 0:
                    pe.wait_ge(late_setup, 1)
                    pe.wait_ge(relu_done, RG * CHUNKS)
                    pe.wait_ge(scores_kept, CHUNKS)
                    pe.wait_ge(table_done, CHUNKS)
                else:
                    pe.wait_ge(mix_done, f)
                for b in range(2):
                    r = 2 * g + b
                    for src, w, n, to in ((agg, wgc, D + 2, bank[b]), (eagg, wsa, D + 1, bank[2 + b])):
                        for h in range(2):
                            mm = pe.matmul(to[:, 0:n], step_of(src[:, h, :], r), w[:, h, :],
                                           start=(h == 0), stop=(h == 1))
                    mm.then_inc(proj, 1)

            def degree_chunk(s, it):
                for u in range(s.units):
                    if u == 4 * (s.q - 1):
                        pe.wait_ge(sta_ready, s.q)
                    adj_unit(s, it, u)

            for s in degree:
                if s.q == 1:
                    degree_chunk(s, 0)
                    degree_chunk(s, 1)
                elif s.units:
                    with pe.Fori(0, 2) as it:
                        degree_chunk(s, it)
                pe.wait_ge(deg_read, 2 * s.q + 2)
                if s.q == 0:
                    pe.wait_ge(consts, N_CONSTS)
                pe.matmul(bank[3][:, 0:2 * BLOCKS], fold_sb[:], deg_sum.rearrange("p i g -> p (i g)"),
                          start=True, stop=True).then_inc(deg_folded, 1)

            def final_chunk(s, it, prev):
                for u in range(s.units):
                    if s.q == 0 and prev is None and u == 4 * (PAIRS - 1):
                        pe.wait_ge(sta_ready, PAIRS)
                    adj_unit(s, it, u)
                    if prev is not None:
                        tail_one(prev, s.units, u)

            pe.wait_ge(setup, 1)
            final_chunk(final[0], 0, None)
            final_chunk(final[0], 1, 0)
            for s in final[1:3]:
                with pe.Fori(0, 2) as it:
                    final_chunk(s, it, 2 * s.q + it - 1)
            final_chunk(final[3], 0, 5)
            final_chunk(final[3], 1, 6)

            def attend_chunk(c, tail):
                for u in range(attend.units):
                    if isinstance(c, int) and c == 0 and u % 2 == 0:
                        pe.wait_ge(sta_ready, PAIRS + u // 2 + 1)
                    adj_unit(attend, c, u)
                    pe.wait_ge(elo_ready, ALL_UNITS * c + u + 1)
                    product(attend, u, c, e_hi, e_lo, acc[2:4], u % 2, ehalf0, pe_e)
                    if tail == "layer one":
                        tail_one(CHUNKS - 1, attend.units, u)
                    for g in range(HALVES):
                        if tail == "layer two" and OUT_AT[g] == u:
                            project_out(c - 1, g)

            attend_chunk(0, "layer one")
            attend_chunk(1, "layer two")
            with pe.Fori(2, CHUNKS) as c:
                attend_chunk(c, "layer two")
            for g in range(HALVES):
                project_out(CHUNKS - 1, g)

        @block.vector
        def _(dve):
            def settle(src, a, b):
                dve.tensor_scalar(a, src, 1, None, ALU.logical_shift_right)
                dve.drain()
                dve.tensor_scalar(b, a, -1.0, float(RSQRT_SEED), ALU.mult, ALU.add)

            def transpose_unit(s, it, u, diagonal):
                n = s.unit(it, u)
                k = s.places[u // 2] if u < s.units else len(s.loaded)
                slot = k % s.slots
                arrived = s.arrivals(it, k)
                if u % 2 == 0:
                    dve.wait_ge(raw_full[slot], 64 * arrived)
                if diagonal is not None:
                    for a in range(QUADS):
                        at = slot * BLOCKS * P + RG * a * P
                        d = raw[QP * a:QP * a + QP, at:at + RG * (P + QP)].rearrange(
                            "p (r j) -> p r j", r=RG)[:, :, 0:QP]
                        i = pick[QP * a:QP * a + QP, bass.ds(diagonal, 1), :].rearrange(
                            "p o (r j) -> p (o r) j", r=RG)
                        dve.tensor_tensor(d, d, i, ALU.add)
                    dve.drain()
                if not (isinstance(n, int) and n < 2):
                    dve.wait_ge(hi_ready, n - 1)
                    dve.wait_ge(lo_ready, n - 1)
                if s.kind == "attend":
                    m = ALL_UNITS * it + u
                    if not (isinstance(m, int) and m < 2):
                        dve.wait_ge(e_ready, m - 1)
                src = raw_t[slot].rearrange("p (g s j) -> p s g j", g=BLOCKS, s=RG)[:, 2 * (u % 2):2 * (u % 2) + 2]
                dve.transpose(adjt[:, u % 2].rearrange("p s (g i) -> p s g i", i=QP), src).then_inc(adjt_ready, 1)
                if s.kind == "degree" and u % 2:
                    dve.drain()
                    dve.nop().then_inc(read_out[slot], READS - 2)

            def low_part(s, it, u):
                n = s.unit(it, u)
                dve.wait_ge(hi_ready, n + 1)
                if not (isinstance(n, int) and n < 2):
                    dve.wait_ge(pe_adj, n - 1)
                b = u % 2
                dve.tensor_tensor(adj_lo[:, b], adjt[:, b], adj_hi[:, b].bitcast(F32), ALU.subtract).then_inc(lo_ready, 1)

            def masked(c, u):
                n, b = ALL_UNITS * c + u, u % 2
                dve.wait_ge(ex_ready, 2 * (n + 1))
                dve.wait_ge(adjt_ready, attend.unit(c, u) + 1)
                if not (isinstance(n, int) and n < 2):
                    dve.wait_ge(ehi_ready, n - 1)
                    dve.wait_ge(elo_ready, n - 1)
                dve.scalar_tensor_tensor(out=eb(b), in0=adjt[:, b], scalar=0.0, in1=exb(b),
                                         op0=ALU.not_equal, op1=ALU.mult).then_inc(e_ready, 1)

            def e_low(c, u):
                n, b = ALL_UNITS * c + u, u % 2
                dve.wait_ge(ehi_ready, n + 1)
                if not (isinstance(n, int) and n < 2):
                    dve.wait_ge(pe_e, n - 1)
                dve.tensor_tensor(e_lo[:, b], eb(b), e_hi[:, b].bitcast(F32), ALU.subtract).then_inc(elo_ready, 1)

            def newton(v, y, t):
                for _ in range(NEWTON):
                    dve.scalar_tensor_tensor(out=t, in0=y, scalar=-0.5, in1=y, op0=ALU.mult, op1=ALU.mult)
                    dve.drain()
                    dve.tensor_tensor(t, t, v, ALU.mult)
                    dve.drain()
                    dve.scalar_tensor_tensor(out=y, in0=t, scalar=1.5, in1=y, op0=ALU.add, op1=ALU.mult)
                    dve.drain()

            def degree_chunk(s, it, head, more):
                for k in range(TILES):
                    if k in s.places:
                        v = 2 * s.places.index(k)
                        if k or head:
                            transpose_unit(s, it, v, None)
                            transpose_unit(s, it, v + 1, None)
                            low_part(s, it, v)
                            low_part(s, it, v + 1)
                    else:
                        mine = slice(BY_ACT[False] + BY_POOL[False] if s.q else 0, BLOCKS)
                        dve.wait_ge(raw_full[k % SLOTS], 64 * s.arrivals(it, k))
                        dve.tensor_reduce(deg_part[:, mine, k], raw_t[k % SLOTS].rearrange("p (g j) -> p g j", g=BLOCKS)[:, mine],
                                          AX_X, ALU.add).then_inc(read_out[k % SLOTS], READS - 2 if s.q else READS)
                for k in range(TILES - SLOTS, TILES):
                    dve.wait_ge(read_out[k % SLOTS], READS * s.arrivals(it, k))
                if s.q:
                    dve.wait_ge(pool_sums, TILES * (2 * (s.q - 1) + it + 1))
                dve.wait_ge(consts, N_CONSTS)
                dve.tensor_reduce(deg_sum[:, bass.ds(it, 1), :].rearrange("p o g -> p (o g)"), deg_part,
                                  AX_X, ALU.add).then_inc(deg_read, 1)
                dve.drain()
                if more:
                    transpose_unit(s, it, s.units, None)
                    transpose_unit(s, it, s.units + 1, None)
                if s.units:
                    dve.wait_ge(half0, s.pass0 + it + 1)
                    dve.wait_ge(consts, N_CONSTS)
                    kept = room[:, bass.ds(2 * s.q + it, 1), :].rearrange("p o n -> p (o n)")
                    dve.tensor_copy(kept[:, 0:COLS], acc[0][:]).then_inc(kept0, 1)
                    dve.wait_ge(pe_adj, s.unit(it, s.units))
                    dve.wait_ge(consts, N_CONSTS)
                    dve.tensor_copy(kept[:, COLS:2 * COLS], acc[1][:]).then_inc(kept1, 1)
                if more:
                    low_part(s, it, s.units)
                    low_part(s, it, s.units + 1)

            def prepare_weights():
                dve.tensor_copy(pick[:, 0, :], fold_sb[:])
                dve.memset(pick[:, 1, :], 0.0)
                dve.tensor_copy(pick[:, 2, :], fold_sb[:])
                for h in range(2):
                    for side, col in ((1, 0), (0, 1)):
                        dve.tensor_tensor_reduce(out=products, in0=wsa[:, h, 0:D], in1=a_row[:, side, :],
                                                 scale=1.0, scalar=0.0, op0=ALU.mult, op1=ALU.add,
                                                 accum_out=w4[:, h, col:col + 1])
                        dve.drain()
                    dve.tensor_scalar(wl_rep[:, h, :], fold_sb[:], 0.0, w4[:, h, 1:2], ALU.mult, ALU.add)
                    dve.tensor_tensor(wsa[:, h, 0:D], wsa[:, h, 0:D], row_s, ALU.subtract)
                dve.memset(wsa[:, 0, D:D + 1], 0.0)
                dve.tensor_copy(wsa[:, 1, D:D + 1], eye_sb[:, P - 1:P])
                dve.drain()
                dve.nop().then_inc(setup, 1)

            def degree_roots(q):
                dve.wait_ge(deg_folded, q + 1)
                for a in range(QUADS):
                    rows = slice(QP * a, QP * a + QP)
                    dve.tensor_scalar(degp1[rows].rearrange("p (i r) -> p i r", i=2),
                                      bank[3][rows, 0:2 * BLOCKS].rearrange("p (i g) -> p i g", i=2)[:, :, RG * a:RG * a + RG],
                                      1.0, None, ALU.add)
                dve.drain()
                dv = dinv[:, 8 * q:8 * q + 8]
                settle(degp1[:].bitcast(I32), seed[:], dv.bitcast(I32))
                dve.drain()
                newton(degp1[:], dv, tmp_d[:])
                dve.nop().then_inc(dinv_done, 1)

            def stationary_low(steps):
                dve.wait_ge(*x_of(steps[0] // 8))
                for st in steps:
                    dve.wait_ge(stahi_ready, st + 1)
                    ins = dve.scalar_tensor_tensor(out=sta_lo[:, st, :], in0=nodes[:, st, :], scalar=dinv[:, st:st + 1],
                                                   in1=sta_hi[:, st, :].bitcast(F32), op0=ALU.mult, op1=ALU.subtract)
                if st % 8 == 7:
                    ins.then_inc(sta_ready, 1)

            for s in degree:
                if s.q == 0:
                    degree_chunk(s, 0, False, False)
                    prepare_weights()
                    degree_chunk(s, 1, False, False)
                elif s.q == 2:
                    with dve.Fori(0, 2) as it:
                        degree_chunk(s, it, False, True)
                else:
                    degree_chunk(s, 0, s.q == 1, True)
                    degree_chunk(s, 1, False, s.q == 1)
                if s.q < PAIRS - 1:
                    degree_roots(s.q)
                    stationary_low(list(range(8 * s.q, 8 * s.q + 8)))
                else:
                    transpose_unit(final[0], 0, 0, 0)
                    transpose_unit(final[0], 0, 1, None)
                    low_part(final[0], 0, 0)

            def chunk_statistics():
                dve.drain()
                dve.tensor_scalar(varc[:], mv[:, :, 1], EPS, None, ALU.add)
                dve.drain()
                settle(varc[:].bitcast(I32), seed_v[:], rstd[:].bitcast(I32))
                dve.drain()
                dve.nop().then_inc(seed_done, 1)

            def row_statistics(f, r):
                dve.wait_ge(sum_done, f + 1)
                dve.bn_stats(stats[:, r, :], val[:, r, :])
                dve.drain()
                dve.bn_aggr(mv[:, r, :], stats[:, r, :])

            def chunk_dinv(c):
                if not (isinstance(c, int) and c == 0):
                    dve.wait_ge(relu_done, RG * c)
                dve.tensor_copy(dinv_c[:], dinv[:, bass.ds(RG * c, RG)]).then_inc(dinvc_ready, 1)

            def residual(c, r):
                if r == 0 and not (isinstance(c, int) and c == 0):
                    dve.wait_ge(norm_done, c)
                row_statistics(RG * c + r, r)
                if r == RG - 1:
                    chunk_statistics()

            def keep_table(c):
                dve.wait_ge(dots_done, RG * c + RG)
                dve.wait_ge(setup, 1)
                dots = bank[2][:, D:D + 4 * RG].rearrange("p (r k) -> p k r", r=RG)
                dve.tensor_copy(table[:, :, bass.ds(RG * c, RG)], dots)
                dve.tensor_scalar(sl_scaled[:, bass.ds(RG * c, RG)], dots[:, 0, :], -SLOPE, None, ALU.mult).then_inc(table_done, 1)

            def x1_low(c, unused_from):
                dve.wait_ge(x1hi_ready, c + 1)
                dve.wait_ge(pe_adj, unused_from)
                lo = steps_of(sta_lo, c)
                dve.tensor_tensor(lo[:, :, 0:D - 1], steps_of(nodes, c)[:, :, 0:D - 1],
                                  steps_of(sta_hi, c)[:, :, 0:D - 1].bitcast(F32), ALU.subtract)
                dve.tensor_scalar(lo[:, :, D - 1], steps_of(nodes, c)[:, :, D - 1], 0.0, None,
                                  ALU.mult).then_inc(sta_ready, 1)

            def tail_one(prev, u, units):
                if TAIL[units]["project"][0] == u:
                    chunk_dinv(prev)
                for r in range(RG):
                    if TAIL[units]["residual"][r] == u:
                        residual(prev, r)

            def final_chunk(s, it, prev, next_pick):
                for u in range(s.units):
                    if u:
                        low_part(s, it, u)
                    if u + 2 < s.units:
                        transpose_unit(s, it, u + 2, 1 + it if u == 0 else None)
                    elif s.q == 3 and next_pick is None:
                        transpose_unit(attend, 0, u + 2 - s.units, None)
                    else:
                        transpose_unit(s, it, u + 2, next_pick if u + 2 == s.units else None)
                    if s.q == 0 and prev is None:
                        if u == 1:
                            degree_roots(PAIRS - 1)
                        if 3 <= u < 7:
                            stationary_low([8 * (PAIRS - 1) + 2 * (u - 3) + i for i in range(2)])
                    if s.q and u == TAIL[s.units]["x1"] + 1:
                        x1_low(2 * (s.q - 1) + it, s.unit0)
                    if prev is not None:
                        tail_one(prev, u, s.units)
                        if TAIL[s.units]["table"] == u and u < s.units - 1:
                            keep_table(prev)
                if s.q == 3 and next_pick is None:
                    low_part(attend, 0, 0)
                    masked(0, 0)
                else:
                    low_part(s, it, s.units)
                dve.wait_ge(half0, s.pass0 + it + 1)
                if prev is not None or s.q:
                    dve.wait_ge(proj, RG * (2 * s.q + it))
                c = 2 * s.q + it
                part = room[:, bass.ds(c, 1), :].rearrange("p o n -> p (o n)")
                if s.q:
                    dve.tensor_tensor(by_step(agg[:, 0, :]), by_column(acc[0][:]), by_column(part[:, 0:COLS]), ALU.add).then_inc(kept0, 1)
                else:
                    dve.tensor_copy(by_step(agg[:, 0, :]), by_column(acc[0][:])).then_inc(kept0, 1)
                dve.wait_ge(pe_adj, s.unit(it, s.units))
                if s.q:
                    dve.tensor_tensor(by_step(agg[:, 1, :]), by_column(acc[1][:]), by_column(part[:, COLS:2 * COLS]), ALU.add).then_inc(kept1, 1)
                else:
                    dve.tensor_copy(by_step(agg[:, 1, :]), by_column(acc[1][:])).then_inc(kept1, 1)
                if prev is not None and TAIL[s.units]["table"] == s.units - 1:
                    keep_table(prev)

            final_chunk(final[0], 0, None, 1)
            final_chunk(final[0], 1, 0, 0)
            for s in final[1:3]:
                with dve.Fori(0, 2) as it:
                    final_chunk(s, it, 2 * s.q + it - 1, 1 + it)
            final_chunk(final[3], 0, 5, 1)
            final_chunk(final[3], 1, 6, None)

            def logits(c, g):
                if g == 0:
                    if not (isinstance(c, int) and c == 0):
                        dve.wait_ge(gates_done, HALVES * c)
                    dve.tensor_tensor(tab_c[:, :, 1:3], table[:, 2:4, bass.ds(RG * c, RG)].rearrange("p k r -> p r k"),
                                      bias_ab[:].unsqueeze(1).broadcast_to((P, RG, 2)), ALU.add)
                    dve.tensor_copy(tab_c[:, :, 0], table[:, 1, bass.ds(RG * c, RG)])
                    dve.drain()
                    dve.nop().then_inc(tabc_done, 1)
                dve.wait_ge(proj, RG * (CHUNKS + c) + 2 * g + 2)
                for b in range(2):
                    r = 2 * g + b
                    ins = dve.tensor_tensor(gate[:, r, 0:2], bank[b][:, D:D + 2], tab_c[:, r, 1:3], ALU.add)
                ins.then_inc(logit_done, 1)

            def use_gates(c, g):
                f, pair = HALVES * c + g, slice(2 * g, 2 * g + 2)
                dve.wait_ge(gates_done, f + 1)
                dve.tensor_scalar(gate[:, pair, 0:2], gate[:, pair, 2:4], 0.5, 0.5, ALU.mult, ALU.add)
                for b in range(2):
                    r = 2 * g + b
                    dve.scalar_tensor_tensor(out=gate[:, r, 4:5], in0=tab_c[:, r, 0:1], scalar=EPS,
                                             in1=bank[2 + b][:, D:D + 1], op0=ALU.mult, op1=ALU.add)
                if not (isinstance(f, int) and f == 0):
                    dve.wait_ge(squashed, f)
                for b in range(2):
                    dve.tensor_tensor(mix[:, b, :], bank[b][:, 0:D], bias_g, ALU.add)
                dve.drain()
                dve.reciprocal(gate[:, pair, 5], gate[:, pair, 4])
                for b in range(2):
                    dve.tensor_scalar(mix[:, b, :], mix[:, b, :], gate[:, 2 * g + b, 1:2], None, ALU.mult)

            def mix_in(c, g):
                pair = slice(2 * g, 2 * g + 2)
                dve.drain()
                dve.tensor_tensor(gate[:, pair, 6], gate[:, pair, 5], gate[:, pair, 0], ALU.mult)
                dve.drain()
                for b in range(2):
                    ins = dve.scalar_tensor_tensor(out=mix[:, b, :], in0=bank[2 + b][:, 0:D],
                                                   scalar=gate[:, 2 * g + b, 6:7], in1=mix[:, b, :],
                                                   op0=ALU.mult, op1=ALU.add)
                ins.then_inc(mix_done, 1)

            def norm_in(c, g):
                if g == 0:
                    dve.wait_ge(norm_done, CHUNKS + c)
                dve.wait_ge(sum_done, RG * CHUNKS + HALVES * c + g + 1)
                for r in (2 * g, 2 * g + 1):
                    dve.bn_stats(stats[:, r, :], val[:, r, :])
                dve.drain()
                for r in (2 * g, 2 * g + 1):
                    dve.bn_aggr(mv[:, r, :], stats[:, r, :])
                if g == HALVES - 1:
                    chunk_statistics()

            def attend_chunk(c, tail, more):
                for u in range(attend.units):
                    if u:
                        masked(c, u)
                        low_part(attend, c, u)
                        if u + 2 < attend.units or more:
                            transpose_unit(attend, c, u + 1 if u == 1 else u + 2, None)
                    e_low(c, u)
                    if u == 1:
                        transpose_unit(attend, c, u + 2, None)
                    if tail == "layer one":
                        tail_one(CHUNKS - 1, u, attend.units)
                        if u == TAIL[attend.units]["table"]:
                            keep_table(CHUNKS - 1)
                        for last, at in X1_LAST:
                            if u == at + 1:
                                x1_low(last, attend.unit0)
                    if tail == "layer two":
                        for g in range(HALVES):
                            if u == OUT_AT[g] + LOGITS:
                                logits(c - 1, g)
                            if u == OUT_AT[g] + GATES_USED:
                                use_gates(c - 1, g)
                            if u == OUT_AT[g] + MIX:
                                mix_in(c - 1, g)
                            if u == OUT_AT[g] + STATISTICS:
                                norm_in(c - 1, g)
                if more:
                    masked(c, attend.units)
                    low_part(attend, c, attend.units)
                dve.wait_ge(pe_adj, attend.unit(c, attend.units))
                dve.wait_ge(proj, RG * (CHUNKS + c))
                dve.tensor_copy(by_step(agg[:, 1, :]), by_column(acc[1][:])).then_inc(kept1, 1)
                dve.wait_ge(pe_e, ALL_UNITS * (c + 1))
                dve.tensor_copy(by_step(eagg[:, 1, :]), by_column(acc[3][:])).then_inc(ekept1, 1)

            attend_chunk(0, "layer one", True)
            dve.wait_ge(late_in, N_LATE)
            for h in range(2):
                dve.tensor_tensor(wgc[:, h, 0:D], wgc[:, h, 0:D], row_g, ALU.subtract)
                dve.tensor_tensor(wgc[:, h, D:D + 2], wgc[:, h, D:D + 2], row_gates[:], ALU.subtract)
            dve.drain()
            dve.nop().then_inc(late_setup, 1)
            attend_chunk(1, "layer two", True)
            with dve.Fori(2, CHUNKS - 1) as c:
                attend_chunk(c, "layer two", True)
            attend_chunk(CHUNKS - 1, "layer two", False)
            for g in range(HALVES):
                logits(CHUNKS - 1, g)
                use_gates(CHUNKS - 1, g)
                mix_in(CHUNKS - 1, g)
                norm_in(CHUNKS - 1, g)

        @block.scalar
        def _(act):
            act.preload_act_table(ACT.Exp)
            def load_x(c, arrived):
                for a in range(QUADS):
                    act.dma_start(nodes[QP * a:QP * a + QP, bass.ds(RG * c, RG), :],
                                  x_v[a][:, bass.ds(c, 1)].rearrange("p o r d -> p (o r) d")).then_inc(arrived, 16)

            small = [
                (fold_sb[:], fold), (eye_sb[:], eye),
                (w0_sb, w0.rearrange("(h p) n -> p h n", h=2)),
                (wsa[:, :, 0:D], w_sa.rearrange("(h p) n -> p h n", h=2)),
                (row_s, w_sa[D - 1, :].partition_broadcast(P)),
                (a_row, a_sa.rearrange("o (h n) -> o h n", h=2)[0].partition_broadcast(P)),
                (bias_ab[:, 0:1], ba.partition_broadcast(P)),
                (bias_ab[:, 1:2], bb.partition_broadcast(P)),
            ]
            for g, w in enumerate((wa, wb)):
                w_v = w.rearrange("o (k h p) -> k h p o", k=2, h=2)
                small.append((row_gates[:, g:g + 1], w[0, D - 1:D].partition_broadcast(P)))
                for h in range(2):
                    small.append((w4[:, h, 2 + g:3 + g], w_v[1, h]))
            for dst, src in small:
                act.dma_start(dst, src).then_inc(consts, 16)
            for c in range(2):
                load_x(c, x_first)

            unread = [bank[b][:, g * P:(g + 1) * P] for b in range(3) for g in range(4)]

            def high_part(s, it, u):
                n, b = s.unit(it, u), u % 2
                act.wait_ge(adjt_ready, n + 1)
                if not (isinstance(n, int) and n < 2):
                    act.wait_ge(pe_adj, n - 1)
                act.activation(adj_hi[:, b], adjt[:, b], ACT.Copy).then_inc(hi_ready, 1)

            def degree_chunk(s, it, head, more):
                for k in range(TILES):
                    products = k in s.places
                    if products and (k or head):
                        high_part(s, it, 2 * s.places.index(k))
                        high_part(s, it, 2 * s.places.index(k) + 1)
                    act.wait_ge(deg_read, 2 * s.q + it)
                    act.wait_ge(raw_full[k % SLOTS], 64 * s.arrivals(it, k))
                    rows = raw_t[k % SLOTS].rearrange("p (g j) -> p g j", g=BLOCKS)
                    for g in range(BY_ACT[products]):
                        ins = act.activation(unread[g], rows[:, g, :], ACT.Copy, accum_out=deg_part[:, g, k:k + 1])
                    ins.then_inc(read_out[k % SLOTS], 1)
                    act.drain()
                    if head and 2 <= k + 1 < CHUNKS:
                        load_x(k + 1, x_in)
                if more:
                    high_part(s, it, s.units)
                    high_part(s, it, s.units + 1)

            def stationary_high(q):
                act.wait_ge(dinv_done, q + 1)
                act.wait_ge(*x_of(q))
                for st in range(8 * q, 8 * q + 8):
                    act.activation(sta_hi[:, st, :], nodes[:, st, :], ACT.Copy,
                                   scale=dinv[:, st:st + 1]).then_inc(stahi_ready, 1)

            for s in degree:
                if s.q == 2:
                    with act.Fori(0, 2) as it:
                        degree_chunk(s, it, False, True)
                elif s.q:
                    degree_chunk(s, 0, s.q == 1, True)
                    degree_chunk(s, 1, False, s.q == 1)
                if s.q == PAIRS - 1:
                    high_part(final[0], 0, 0)
                else:
                    stationary_high(s.q)
            def relu(c, r):
                f = RG * c + r
                act.wait_ge(proj, f + 1)
                if r == 0:
                    act.wait_ge(dinvc_ready, c + 1)
                if not (isinstance(f, int) and f < 2):
                    act.wait_ge(sum_done, f - 1)
                act.activation(relu_sb[:, r % 2, :], bank[r % 2][:, 0:D], ACT.Relu,
                               scale=dinv_c[:, r:r + 1]).then_inc(relu_done, 1)

            def keep_x1t(c, r):
                f = RG * c + r
                act.wait_ge(xt_done, f + 1)
                if not (isinstance(f, int) and f < 2):
                    act.wait_ge(dots_done, f - 1)
                act.activation(x1t[:, r % 2], turned[r % 2][:, 0:D].rearrange("p (h k) -> p h k", h=2),
                               ACT.Copy).then_inc(xt_kept, 1)

            def keep_scores(c):
                act.wait_ge(dots_done, RG * c + RG)
                act.wait_ge(setup, 1)
                act.activation(room[:, bass.ds(c, 1), 0:COLS].rearrange("p o n -> p (o n)"), bank[3][:],
                               ACT.Copy).then_inc(scores_kept, 1)

            def normalise(count):
                act.wait_ge(root_done, count)
                for r in range(RG):
                    ins = act.activation(val[:, r, :], val[:, r, :], ACT.Identity, bias=shift[:, r:r + 1],
                                         scale=rstd[:, r:r + 1])
                ins.then_inc(norm_done, 1)

            def tail_one(prev, u, units):
                for r in range(RG):
                    if TAIL[units]["relu"][r] == u:
                        relu(prev, r)
                if TAIL[units]["norm"] == u:
                    normalise(prev + 1)
                    act.wait_ge(norm_done, prev + 1)
                    act.wait_ge(setup, 1)
                    rows = nodes[:].rearrange("p (c r) d -> p c (r d)", r=RG)[:, bass.ds(prev, 1), :]
                    act.activation(rows.rearrange("p o n -> p (o n)"), val[:].rearrange("p r d -> p (r d)"),
                                   ACT.Copy).then_inc(nodes_done, 1)
                for r in range(RG):
                    if TAIL[units]["keep"][r] == u:
                        keep_x1t(prev, r)
                if TAIL[units]["table"] == u:
                    keep_scores(prev)

            def x1_high(c, unused_from):
                act.wait_ge(nodes_done, c + 1)
                act.wait_ge(pe_adj, unused_from)
                hi = steps_of(sta_hi, c)
                act.activation(hi[:, :, 0:D - 1], steps_of(nodes, c)[:, :, 0:D - 1], ACT.Copy)
                act.activation(hi[:, :, D - 1], steps_of(nodes, c)[:, :, D - 1], ACT.Copy, scale=0.0,
                               bias=1.0).then_inc(x1hi_ready, 1)

            def final_chunk(s, it, prev):
                for u in range(s.units):
                    high_part(s, it, u + 1)
                    if s.q == 0 and prev is None and u == 2:
                        stationary_high(PAIRS - 1)
                    if s.q and u == TAIL[s.units]["x1"]:
                        x1_high(2 * (s.q - 1) + it, s.unit0)
                    if prev is not None:
                        tail_one(prev, u, s.units)

            final_chunk(final[0], 0, None)
            final_chunk(final[0], 1, 0)
            for s in final[1:3]:
                with act.Fori(0, 2) as it:
                    final_chunk(s, it, 2 * s.q + it - 1)
            def next_scores(c):
                act.wait_ge(scores_kept, min(c, CHUNKS) + 1 if isinstance(c, int) else c + 1)
                if not (isinstance(c, int) and c == 0):
                    act.wait_ge(ex_mid, 2 * ALL_UNITS * c)
                act.wait_ge(setup, 1)
                act.activation(sl_chunk, room[:, bass.ds(c, 1), 0:COLS].rearrange("p o n -> p (o n)"), ACT.Copy)
                act.drain()

            def exponent(n, b, steps):
                if not (isinstance(n, int) and n < 2):
                    act.wait_ge(elo_ready, n - 1)
                for j, st in enumerate(steps):
                    act.activation(exb(b)[:, j, :], sl_chunk, ACT.Relu, bias=table[:, 0, st:st + 1]).then_inc(ex_mid, 1)
                act.wait_ge(ex_mid, 2 * (n + 1))
                for j, st in enumerate(steps):
                    act.activation(exb(b)[:, j, :], exb(b)[:, j, :], ACT.Exp, bias=sl_scaled[:, st:st + 1],
                                   scale=-(1 - SLOPE)).then_inc(ex_ready, 1)

            final_chunk(final[3], 0, 5)
            act.wait_ge(kept1, LAYER1_PASSES + 2 * (PAIRS - 1))
            next_scores(0)
            exponent(0, 0, [attend.step(0, j) for j in range(2)])
            final_chunk(final[3], 1, 6)

            def e_high(c, u):
                n, b = ALL_UNITS * c + u, u % 2
                act.wait_ge(e_ready, n + 1)
                if not (isinstance(n, int) and n < 2):
                    act.wait_ge(pe_e, n - 1)
                act.activation(e_hi[:, b], eb(b), ACT.Copy).then_inc(ehi_ready, 1)

            def gates(c, g):
                if g == 0:
                    act.wait_ge(tabc_done, c + 1)
                    act.activation(tab_c[:, :, 0], tab_c[:, :, 0], ACT.Exp, scale=SLOPE)
                act.wait_ge(logit_done, HALVES * c + g + 1)
                act.activation(gate[:, 2 * g:2 * g + 2, 2:4], gate[:, 2 * g:2 * g + 2, 0:2], ACT.Tanh,
                               scale=0.5).then_inc(gates_done, 1)

            def squash(c, g):
                f = HALVES * c + g
                act.wait_ge(mix_done, f + 1)
                if not (isinstance(f, int) and f == 0):
                    act.wait_ge(sum_done, RG * CHUNKS + f)
                act.activation(zed, mix, ACT.Tanh, scale=0.5)
                act.drain()
                act.activation(zed, zed, ACT.Copy, scale=0.5, bias=0.5).then_inc(squashed, 1)

            def attend_chunk(c, tail, more):
                for u in range(attend.units):
                    e_high(c, u)
                    if u + 1 < attend.units:
                        exponent(ALL_UNITS * c + u + 1, (u + 1) % 2, [attend.step(u + 1, j) for j in range(2)])
                        high_part(attend, c, u + 1)
                    elif more:
                        next_scores(c + 1)
                        exponent(ALL_UNITS * (c + 1), 0, [attend.step(0, j) for j in range(2)])
                        high_part(attend, c + 1, 0)
                    if tail == "layer one":
                        tail_one(CHUNKS - 1, u, attend.units)
                        for last, at in X1_LAST:
                            if u == at:
                                x1_high(last, attend.unit0)
                    if tail == "layer two":
                        for g in range(HALVES):
                            if u == OUT_AT[g] + GATES:
                                gates(c - 1, g)
                            if u == OUT_AT[g] + SQUASH:
                                squash(c - 1, g)
                        if u == 0 and not (isinstance(c, int) and c == 1):
                            normalise(CHUNKS + c - 1)
                p = attend.pass0 + c + 1
                act.wait_ge(half0, p)
                act.wait_ge(proj, RG * (CHUNKS + c))
                act.activation(by_step(agg[:, 0, :]), by_column(acc[0][:]), ACT.Copy).then_inc(kept0, 1)
                act.wait_ge(ehalf0, c + 1)
                act.activation(by_step(eagg[:, 0, :]), by_column(acc[2][:]), ACT.Copy).then_inc(ekept0, 1)

            attend_chunk(0, "layer one", True)
            attend_chunk(1, "layer two", True)
            with act.Fori(2, CHUNKS - 1) as c:
                attend_chunk(c, "layer two", True)
            attend_chunk(CHUNKS - 1, "layer two", False)
            normalise(2 * CHUNKS - 1)
            for g in range(HALVES):
                gates(CHUNKS - 1, g)
                squash(CHUNKS - 1, g)
            normalise(2 * CHUNKS)

        @block.gpsimd
        def _(pool):
            def root(count):
                pool.wait_ge(seed_done, count)
                for _ in range(NEWTON):
                    pool.tensor_tensor(tmp_v[:], rstd[:], rstd[:], ALU.mult)
                    pool.drain()
                    pool.tensor_tensor(tmp_v[:], tmp_v[:], varc[:], ALU.mult)
                    pool.drain()
                    pool.tensor_scalar(tmp_v[:], tmp_v[:], -0.5, 1.5, ALU.mult, ALU.add)
                    pool.drain()
                    pool.tensor_tensor(rstd[:], rstd[:], tmp_v[:], ALU.mult)
                    pool.drain()
                pool.tensor_tensor(shift[:], mv[:, :, 0], rstd[:], ALU.mult)
                pool.drain()
                pool.tensor_scalar(shift[:], shift[:], -1.0, None, ALU.mult).then_inc(root_done, 1)

            def layer_one(c):
                for r in range(RG):
                    f = RG * c + r
                    pool.wait_ge(relu_done, f + 1)
                    if r == 0 and not (isinstance(c, int) and c == 0):
                        pool.wait_ge(dots_done, RG * c)
                        pool.wait_ge(nodes_done, c)
                    pool.wait_ge(x_in, 16 * QUADS * (CHUNKS - 2))
                    pool.tensor_tensor(val[:, r, :], relu_sb[:, r % 2, :],
                                       nodes[:, bass.ds(f, 1), :].rearrange("p o d -> p (o d)"),
                                       ALU.add).then_inc(sum_done, 1)
                root(c + 1)

            def degree_chunk(s, it):
                for k in range(TILES):
                    first = BY_ACT[k in s.places]
                    count = BY_POOL[k in s.places]
                    mine = slice(first, first + count)
                    pool.wait_ge(raw_full[k % SLOTS], 64 * s.arrivals(it, k))
                    rows = raw_t[k % SLOTS].rearrange("p (g j) -> p g j", g=BLOCKS)[:, mine]
                    part = halved[:, 0:count]
                    n = P // 2
                    pool.tensor_tensor(part, rows[:, :, 0:n], rows[:, :, n:P], ALU.add).then_inc(read_out[k % SLOTS], 1)
                    pool.drain()
                    while n > 2:
                        n //= 2
                        pool.tensor_tensor(part[:, :, 0:n], part[:, :, 0:n], part[:, :, n:2 * n], ALU.add)
                        pool.drain()
                    pool.wait_ge(deg_read, 2 * s.q + it)
                    pool.tensor_tensor(deg_part[:, mine, k], part[:, :, 0], part[:, :, 1], ALU.add).then_inc(pool_sums, 1)
                    pool.drain()

            pool.wait_ge(setup, 1)
            degree_chunk(degree[1], 0)
            degree_chunk(degree[1], 1)
            for s in degree[2:]:
                with pool.Fori(0, 2) as it:
                    degree_chunk(s, it)

            layer_one(0)
            with pool.Fori(1, CHUNKS) as c:
                layer_one(c)

            def layer_two(c):
                for g in range(HALVES):
                    pool.wait_ge(squashed, HALVES * c + g + 1)
                    if g == 0:
                        if isinstance(c, int) and c == 0:
                            pool.wait_ge(dots_done, RG * CHUNKS)
                            pool.wait_ge(nodes_done, CHUNKS)
                        else:
                            pool.wait_ge(stored, 16 * QUADS * c)
                    pool.tensor_tensor(val[:, 2 * g:2 * g + 2, :], zed,
                                       nodes[:, bass.ds(RG * c + 2 * g, 2), :], ALU.add).then_inc(sum_done, 1)
                root(CHUNKS + c + 1)

            layer_two(0)
            with pool.Fori(1, CHUNKS) as c:
                layer_two(c)


N_CONSTS = 16 * (8 + 2 * 3)
N_LATE = 16 * (3 + 2 * 2)

_INS = ['x', 'adj', 'L0_gnn_weight', 'L1_gnn_W_sa', 'L1_gnn_a_sa', 'L1_gnn_W_gcnb', 'L1_gnn_b_gcnb',
        'L1_gnn_Wa', 'L1_gnn_ba', 'L1_gnn_Wb', 'L1_gnn_bb']


def kernel(**inputs):
    import numpy as np
    import concourse.bacc as bacc
    from concourse.bass_utils import run_bass_kernel_spmd as run

    nc = bacc.Bacc("TRN2", target_bir_lowering=False, num_devices=1)
    arrays = {name: np.ascontiguousarray(inputs[name]) for name in _INS}
    place = np.arange(P)
    arrays["eye"] = np.eye(P, dtype=np.float32)
    arrays["fold"] = (place[:, None] % QP == place[None, :] % QP).astype(np.float32)
    args = [nc.dram_tensor(f"in_{n}", a.shape, mybir.dt.from_np(a.dtype), kind="ExternalInput").ap()
            for n, a in arrays.items()]
    out = nc.dram_tensor("out_0", arrays["x"].shape, F32, kind="ExternalOutput").ap()
    two_layers(nc, *args, out)
    r = run(nc, [{f"in_{n}": a for n, a in arrays.items()}], core_ids=[0])
    return r.results[0]["out_0"]
```
